# Optimizing a Trainium2 kernel written in Bass

```python
import numpy as np
import jax
import jax.numpy as jnp

def _softmax(x, axis=-1):
    return jax.nn.softmax(x, axis=axis)

def _gelu(x):
    return jax.nn.gelu(x, approximate=True)

def _silu(x):
    return jax.nn.silu(x)

def _sigmoid(x):
    return jax.nn.sigmoid(x)

def _layernorm(x, axis=-1, eps=1e-05):
    m = jnp.mean(x, axis=axis, keepdims=True)
    v = jnp.var(x, axis=axis, keepdims=True)
    return (x - m) / jnp.sqrt(v + eps)

def _scatter_add(tgt, idx, src, axis=0):
    return tgt.at[idx].add(src)

def _segment_sum(src, seg, n):
    return jax.ops.segment_sum(src, seg, n)
kernel_name = 'mk_flamingo_gated_d1_seqx_r2_9602ef'

def setup_inputs(seed: int=0):
    np.random.seed(seed)
    _w = jnp.asarray

    def _rec_inputs():
        import jax
        import jax.numpy as jnp
        _rk = jax.random.key(seed)
        x = 7.22e-05 + 1 * jax.random.normal(jax.random.fold_in(_rk, 1), (4, 1024, 1024), jnp.float32)
        _lenS = 1024 - jax.random.randint(jax.random.fold_in(_rk, 7), (4,), 0, max(1, 1024 // 4) + 1, jnp.int32)
        _lenS2 = 1024 - jax.random.randint(jax.random.fold_in(_rk, 8), (4,), 0, max(1, 1024 // 4) + 1, jnp.int32)
        _ctx_1024P = jax.random.normal(jax.random.fold_in(_rk, 11), (4, 16, 512), jnp.float32)
        _ctx_1024c = jax.random.dirichlet(jax.random.fold_in(_rk, 511), 0.3 * jnp.ones((16,), jnp.float32), (4, 1024))
        _ctx_1024t = jnp.einsum('bsk,bkd->bsd', _ctx_1024c, _ctx_1024P)
        _ctx_1024t = _ctx_1024t * jax.lax.rsqrt(jnp.mean(jnp.square(_ctx_1024t)) + 1e-12) * 0.953939
        ctx_1024 = 2.81802e-05 + 1.00001 * (_ctx_1024t + 0.3 * jax.random.normal(jax.random.fold_in(_rk, 611), (4, 1024, 512), jnp.float32))
        _g = jax.random.normal(jax.random.fold_in(_rk, 9001), (2, 1), jnp.float32)
        _g = jnp.sign(_g) * jnp.maximum(jnp.abs(_g), 1.0) + (_g == 0) * 1.0
        g_xattn = _g[0]
        g_ffn = _g[1]
        return (x, ctx_1024, g_xattn, g_ffn)
    x, ctx_1024, g_xattn, g_ffn = _rec_inputs()

    def _L0_xattn_setup():
        import jax, jax.numpy as jnp
        import numpy as np
        key = jax.random.key(seed)
        ks = jax.random.split(key, 6)
        B, L, N, C, D = (8, 256, 1024, 512, 128)
        return {'teacher_logits': jax.random.normal(ks[0], (B, L, N), dtype=jnp.float32), 'teacher_features': jax.random.normal(ks[1], (B, N, C), dtype=jnp.float32), 'Wq': jax.random.normal(ks[2], (D, C), dtype=jnp.float32) * (1.0 / np.sqrt(C)), 'bq': jnp.zeros((D,), dtype=jnp.float32), 'Wk': jax.random.normal(ks[3], (D, C), dtype=jnp.float32) * (1.0 / np.sqrt(C)), 'bk': jnp.zeros((D,), dtype=jnp.float32)}
    _L0_xattn_all = _L0_xattn_setup()
    _L0_xattn_in = {k: v for k, v in _L0_xattn_all.items() if k in ('Wq', 'bq', 'Wk', 'bk')}
    del _L0_xattn_all

    def _L0_ffn_setup():
        import jax, jax.numpy as jnp
        import numpy as np
        K = 2
        SCALING = 16.0 / 16.0
        key = jax.random.key(seed)
        ks = jax.random.split(key, 7)
        B, T, D, O, E, R = (2, 2048, 1024, 1024, 8, 16)
        return {'x': jax.random.normal(ks[0], (B, T, D), dtype=jnp.float32), 'W': jax.random.normal(ks[1], (O, D), dtype=jnp.float32) * (1.0 / np.sqrt(D)), 'b': jax.random.normal(ks[2], (O,), dtype=jnp.float32) * 0.02, 'lora_A': jax.random.normal(ks[3], (E, R, D), dtype=jnp.float32) * (1.0 / np.sqrt(D)), 'lora_B': jax.random.normal(ks[4], (E, O, R), dtype=jnp.float32) * 0.02, 'gate_w': jax.random.normal(ks[5], (E, D), dtype=jnp.float32) * 0.02, 'gate_b': jax.random.normal(ks[6], (E,), dtype=jnp.float32) * 0.02}
    _L0_ffn_all = _L0_ffn_setup()
    _L0_ffn_in = {k: v for k, v in _L0_ffn_all.items() if k in ('W', 'b', 'lora_A', 'lora_B', 'gate_w', 'gate_b')}
    del _L0_ffn_all
    return {'x': x, 'ctx_1024': ctx_1024, 'g_xattn': g_xattn, 'g_ffn': g_ffn, 'L0_xattn_Wq': _L0_xattn_in['Wq'], 'L0_xattn_bq': _L0_xattn_in['bq'], 'L0_xattn_Wk': _L0_xattn_in['Wk'], 'L0_xattn_bk': _L0_xattn_in['bk'], 'L0_ffn_W': _L0_ffn_in['W'], 'L0_ffn_b': _L0_ffn_in['b'], 'L0_ffn_lora_A': _L0_ffn_in['lora_A'], 'L0_ffn_lora_B': _L0_ffn_in['lora_B'], 'L0_ffn_gate_w': _L0_ffn_in['gate_w'], 'L0_ffn_gate_b': _L0_ffn_in['gate_b']}

def reference(x, ctx_1024, g_xattn, g_ffn, L0_xattn_Wq, L0_xattn_bq, L0_xattn_Wk, L0_xattn_bk, L0_ffn_W, L0_ffn_b, L0_ffn_lora_A, L0_ffn_lora_B, L0_ffn_gate_w, L0_ffn_gate_b):
    import jax
    import jax.numpy as jnp

    def _L0_xattn_ref(teacher_logits, teacher_features, Wq, bq, Wk, bk):
        import jax, jax.numpy as jnp
        import numpy as np
        query = jnp.einsum('bnc,dc->bnd', teacher_features, Wq) + bq
        key = jnp.einsum('bnc,dc->bnd', teacher_features, Wk) + bk
        energy = jnp.einsum('bnd,bmd->bnm', query, key)
        attention = jax.nn.softmax(energy, axis=-1)
        x_m = jnp.einsum('bln,bmn->blm', teacher_logits, attention)
        return x_m

    def _L0_ffn_ref(x, W, b, lora_A, lora_B, gate_w, gate_b):
        import jax, jax.numpy as jnp
        import numpy as np
        K = 2
        SCALING = 16.0 / 16.0
        orig_shape = x.shape
        D = orig_shape[-1]
        O = W.shape[0]
        x_flat = x.reshape(-1, D)
        base = x_flat @ W.T + b
        logits = x_flat @ gate_w.T + gate_b
        topk_logits, topk_idx = jax.lax.top_k(logits, K)
        gates = jax.nn.softmax(topk_logits, axis=-1)
        xA = jnp.einsum('nd,erd->ner', x_flat, lora_A)
        delta_all = jnp.einsum('ner,eor->neo', xA, lora_B)
        delta_topk = jnp.take_along_axis(delta_all, topk_idx[:, :, None], axis=1)
        lora_update = jnp.sum(delta_topk * gates[:, :, None], axis=1)
        out = base + SCALING * lora_update
        return out.reshape(*orig_shape[:-1], O)
    x = x + jnp.tanh(g_xattn[0]) * _L0_xattn_ref(_layernorm(x, axis=-1), ctx_1024, L0_xattn_Wq, L0_xattn_bq, L0_xattn_Wk, L0_xattn_bk)
    x = x + jnp.tanh(g_ffn[0]) * _L0_ffn_ref(_layernorm(x, axis=-1), L0_ffn_W, L0_ffn_b, L0_ffn_lora_A, L0_ffn_lora_B, L0_ffn_gate_w, L0_ffn_gate_b)
    return x

_drawn_inputs = setup_inputs


def setup_inputs(seed=0):
    import zlib

    import numpy as np

    out = dict(_drawn_inputs(seed))
    spreads = {'L0_xattn_bq': (0.0, 0.1), 'L0_xattn_bk': (0.0, 2.0)}
    factors = {'L0_ffn_b': 4.575, 'L0_ffn_gate_b': 29.648}
    for name, (base, spread) in spreads.items():
        noise = np.random.default_rng([zlib.crc32(name.encode()), seed]).standard_normal(out[name].shape)
        drawn = base * np.exp(spread * noise) if base else spread * noise
        out[name] = jnp.asarray(drawn.astype(out[name].dtype))
    for name, factor in factors.items():
        out[name] = (out[name] * factor).astype(out[name].dtype)
    return out
```

```python
from contextlib import ExitStack

import concourse.bass as bass
from concourse import mybir

F32 = mybir.dt.float32
F32R = mybir.dt.float32r
F16 = mybir.dt.float16
U32 = mybir.dt.uint32
I32 = mybir.dt.int32
ALU = mybir.AluOpType
ACT = mybir.ActivationFunctionType
AX = mybir.AxisListType
RMAX = bass.bass_isa.ReduceOp.max

P = 128
BANK = 512
B, L, D = 4, 1024, 1024
N, C, DH = 1024, 512, 128
EX, R = 8, 16
ER = EX * R
EPS = 1e-5

TILES = L // P
STEPS = B * TILES
KD = D // P
KC = C // P
HB = BANK // P

NORM_SCALE = 2.0 ** 10
PROB_SCALE = 2.0 ** 15
W_TOP = 2.0 ** 14
EXPONENT = 0x7F800000
GATE_LINKS = 11

SEGMENTS = [(0, 0, 2, "project", False), (0, 4, 2, "softmax", True),
            (1, 0, 2, "project", True), (1, 4, 2, "softmax", True),
            (2, 0, 2, "project", True), (2, 4, 2, "softmax", True),
            (3, 0, 3, None, True), (3, 6, 1, None, False)]

PREP = ([("lora_b", 0), ("lora_b", 1), ("lora_a", 0), ("lora_a", 1), ("gate", 0)]
        + [("w", n) for n in range(2 * TILES)])
PREP_AT = {0: [(0, 3), (0, 7)] + [(1, k) for k in range(8)],
           1: [(0, k) for k in range(8)] + [(1, k) for k in range(3)]}
PREP_FIRST = {0: 0, 1: len(PREP_AT[0])}


def run_steps(eng, step, straight=()):
    for n, (b, first, pairs, kind, looped) in enumerate(SEGMENTS):
        base = TILES * b + first
        if looped and n not in straight:
            with eng.Fori(0, pairs) as i:
                for u in range(2):
                    step(base + 2 * i + u, b, kind, i, u)
        else:
            for i in range(pairs):
                for u in range(2):
                    step(base + 2 * i + u, b, kind, i, u)


def wait(eng, sem, value):
    if isinstance(value, int) and value <= 0:
        return
    eng.wait_ge(sem, value)


def at_least(s, n):
    return not isinstance(s, int) or s >= n


def flamingo_block(nc, x, ctx_tokens, g_xattn, g_ffn, Wq, bq, Wk, bk, W, bias, lora_A, lora_B,
                   gate_w, gate_b, out):
    x_tiles = x.rearrange("b (t p) d -> (b t) p d", p=P)
    out_tiles = out.rearrange("b (t p) d -> (b t) p d", p=P)
    ctx_pairs = ctx_tokens.rearrange("b (q t p) c -> (b q) p t c", p=P, t=2)
    PAIRS = B * N // (2 * P)

    with ExitStack() as stack:
        def sb(name, shape, dt):
            return stack.enter_context(nc.sbuf_tensor(name, shape, dt))

        def sem(name):
            return stack.enter_context(nc.semaphore(name))

        attnT = [sb(f"attnT{v}", [P, 2, KD, L], F16) for v in range(2)]
        wT = sb("wT", [P, 2, KD, D], F16)
        agT = sb("agT", [P, 2, KD, ER + EX], F16)
        bT = sb("bT", [P, 2, D], F32R)
        xT = sb("xT", [P, 2, KD, P], F16)
        x1T = sb("x1T", [P, 2, KD, P], F16)
        ctxT = sb("ctxT", [P, 2, KC, BANK], F32R)
        wqkT = sb("wqkT", [P, 2, 2, KC, DH], F32R)
        kT = sb("kT", [P, 2, N], F32R)
        qT = sb("qT", [P, L], F32)
        q_tile = [sb(f"q_tile{v}", [P, 2, P], F32R) for v in range(2)]
        hT = sb("hT", [P, 2, P], F32R)
        ctx_in = [sb(f"ctx_in{u}", [P, 2, C], F32) for u in range(2)]
        x_in = [sb(f"x_in{u}", [P, D], F32) for u in range(2)]
        x_norm = sb("x_norm", [P, D], F32)
        x1 = [sb(f"x1_{u}", [P, D], F32) for u in range(2)]
        x1_norm = sb("x1_norm", [P, D], F32)
        out_row = sb("out_row", [P, D], F32)
        probs = [sb(f"probs{v}", [P, N], F32) for v in range(2)]
        bias_row = sb("bias_row", [P, D], F32)
        ident = sb("ident", [P, P], F32)
        bqk = sb("bqk", [P, 2], F32)
        g_in = sb("g_in", [P, 2], F32)
        tanh_g = sb("tanh_g", [P, 2], F32)
        bound_parts = sb("bound_parts", [P, 8], F32)
        bound = sb("bound", [P, 2], F32)
        bound_all = sb("bound_all", [P, 2], F32)
        bound_low = sb("bound_low", [P, 2], F32)
        pow2 = sb("pow2", [P, 2], F32)
        inv_pow2 = sb("inv_pow2", [P, 2], F32)
        scale = sb("scale", [P, 2], F32)
        attn_coef = sb("attn_coef", [P, 1], F32)
        ffn_coef = sb("ffn_coef", [P, 1], F32)
        logit_coef = sb("logit_coef", [P, 1], F32)
        lora_coef = sb("lora_coef", [P, 1], F32)
        gate_bias = sb("gate_bias", [P, EX], F32)
        iota_i = sb("iota_i", [P, EX], I32)
        iota = sb("iota", [P, EX], F32)
        minus_half = sb("minus_half", [P, 1], F32)
        neg_max = sb("neg_max", [P, 2], F32)
        row_sum = sb("row_sum", [P, 2], F32)
        inv_sum = sb("inv_sum", [P, 2], F32)
        ln = {k: (sb(f"{k}_bn", [P, 12], F32), sb(f"{k}_mv", [P, 2], F32),
                  sb(f"{k}_var", [P, 1], F32), sb(f"{k}_rstd", [P, 1], F32)) for k in ("x", "x1")}
        ga = sb("ga", [P, ER + EX], F32)
        logits = sb("logits", [P, EX], F32)
        top = sb("top", [P, 8], F32)
        top_idx = sb("top_idx", [P, 8], U32)
        top_idx_f = sb("top_idx_f", [P, 2], F32)
        wait_word = sb("wait_word", [P, 1], F32)
        gap = sb("gap", [P, 1], F32)
        gap_exp = sb("gap_exp", [P, 1], F32)
        gate_den = sb("gate_den", [P, 1], F32)
        gate_inv = sb("gate_inv", [P, 1], F32)
        gate_top = sb("gate_top", [P, 2], F32)
        gate_of = sb("gate_of", [P, 3, EX], F32)
        h_row = sb("h_row", [P, ER], F32)

        w_in = attnT[1][:].rearrange("p a k m -> p (a k m)").bitcast(F32) \
            .rearrange("p (t m) -> p t m", t=TILES)
        wqk_in = x1[0][:].rearrange("p (a c) -> p a c", a=2)
        lora_a_in = x1[1]
        gate_in = x1_norm
        lora_b_in = out_row[:].rearrange("p (t e r) -> p t e r", t=TILES, e=EX)

        ps_attn = stack.enter_context(nc.psum_tensor("ps_attn", [P, 2 * BANK], F32))
        ps_ffn = stack.enter_context(nc.psum_tensor("ps_ffn", [P, 2 * BANK], F32))
        ps_score = stack.enter_context(nc.psum_tensor("ps_score", [P, 2 * BANK], F32))
        ps_t = stack.enter_context(nc.psum_tensor("ps_t", [P, 2 * BANK], F32))

        def half(ps, h):
            return ps[:, h * BANK:(h + 1) * BANK]

        def prep_parts(n, part):
            name, at = PREP[n]
            ps = half(ps_t, n % 2)
            if name == "lora_b":
                return bT[:, part, at * BANK:(at + 1) * BANK], ps, "b"
            if name == "lora_a":
                return (agT[:, part, HB * at:HB * at + HB, 0:ER],
                        ps.rearrange("p (k n) -> p k n", k=HB), "a")
            if name == "gate":
                return (agT[:, part, :, ER:ER + EX],
                        ps[:, 0:KD * EX].rearrange("p (k n) -> p k n", k=KD), "a")
            tile, h = at // 2, at % 2
            return (wT[:, part, HB * h:HB * h + HB, tile * P:(tile + 1) * P],
                    ps.rearrange("p (k n) -> p k n", k=HB), "w")

        wqk_loaded, w_loaded, ab_loaded, small_loaded = map(sem, (
            "wqk_loaded", "w_loaded", "ab_loaded", "small_loaded"))
        ctx_loaded = [sem(f"ctx_loaded{u}") for u in range(2)]
        x_loaded = [sem(f"x_loaded{u}") for u in range(2)]
        out_stored = sem("out_stored")
        consts_ready, ident_zero, ident_ready, bias_row_ready = map(sem, (
            "consts_ready", "ident_zero", "ident_ready", "bias_row_ready"))
        tanh_ready, act_bound, dve_bound, bound_reduced, scales_ready = map(sem, (
            "tanh_ready", "act_bound", "dve_bound", "bound_reduced", "scales_ready"))
        wqk_t, wqk_hi, wqk_lo = map(sem, ("wqk_t", "wqk_hi", "wqk_lo"))
        prep_t, prep_hi, prep_lo = map(sem, ("prep_t", "prep_hi", "prep_lo"))
        ctx_t, ctx_hi, ctx_lo = map(sem, ("ctx_t", "ctx_hi", "ctx_lo"))
        k_ready, q_ready, k_hi, k_lo, q_copied = map(sem, (
            "k_ready", "q_ready", "k_hi", "k_lo", "q_copied"))
        q_hi, q_lo, scores_ready, max_ready, exp_ready, inv_ready, probs_ready = map(sem, (
            "q_hi", "q_lo", "scores_ready", "max_ready", "exp_ready", "inv_ready", "probs_ready"))
        probs_t, probs_hi, probs_lo = map(sem, ("probs_t", "probs_hi", "probs_lo"))
        x_t, x_hi, x_lo = map(sem, ("x_t", "x_hi", "x_lo"))
        x1_t, x1_hi, x1_lo = map(sem, ("x1_t", "x1_hi", "x1_lo"))
        attn_ready, x1_half, ffn_ready, out_half = map(sem, (
            "attn_ready", "x1_half", "ffn_ready", "out_half"))
        ln_sem = {k: [sem(f"{k}_{w}") for w in ("bn_ready", "mv_ready", "var_ready", "rstd_ready",
                                                "norm_ready")] for k in ("x", "x1")}
        x1_biased = sem("x1_biased")
        ga_ready, ga_copied, gate_chain, gap_ready, gap_exp_ready, h_ready, h_t, h_hi, h_lo = map(
            sem, ("ga_ready", "ga_copied", "gate_chain", "gap_ready", "gap_exp_ready", "h_ready",
                  "h_t", "h_hi", "h_lo"))
        block = stack.enter_context(nc.Block())

        @block.sync
        def _(sp):
            def load_pair(pair, u):
                sp.dma_start(ctx_in[u][:], ctx_pairs[pair]).then_inc(ctx_loaded[u], 16)

            def load_x(s, u):
                sp.dma_start(x_in[u][:], x_tiles[s]).then_inc(x_loaded[u], 16)

            sp.dma_start(wqk_in[:, 0, :], Wq).then_inc(wqk_loaded, 16)
            sp.dma_start(wqk_in[:, 1, :], Wk).then_inc(wqk_loaded, 16)
            for u in range(2):
                load_pair(u, u)
            for n, v in enumerate((bq, bk)):
                sp.dma_start(bqk[:, n:n + 1], v.rearrange("(p a) -> p a", a=1)) \
                    .then_inc(small_loaded, 16)
            for n, v in enumerate((g_xattn, g_ffn)):
                sp.dma_start(g_in[:, n:n + 1], v.partition_broadcast(P)).then_inc(small_loaded, 16)
            sp.dma_start(gate_bias[:], gate_b.partition_broadcast(P)).then_inc(small_loaded, 16)
            sp.dma_start(bias_row[:], bias.partition_broadcast(P)).then_inc(small_loaded, 16)
            load_x(0, 0)
            for pair in range(2, 6):
                sp.wait_ge(ctx_t, 2 * (pair - 2) + 2)
                load_pair(pair, pair % 2)
            load_x(1, 1)
            for t in range(0, TILES, 4):
                sp.dma_start(w_in[:, t:t + 4, :], W.rearrange("(t p) m -> p t m", p=P)[:, t:t + 4, :]) \
                    .then_inc(w_loaded, 16)
            sp.dma_start(lora_a_in[:], lora_A.rearrange("e r m -> (e r) m")).then_inc(ab_loaded, 16)
            sp.dma_start(gate_in[0:EX, :], gate_w).then_inc(ab_loaded, 16)
            for t in range(TILES):
                sp.dma_start(lora_b_in[:, t], lora_B.rearrange("e (t p) r -> t p e r", p=P)[t]) \
                    .then_inc(ab_loaded, 16)

            def step(s, b, kind, i, u):
                if at_least(s, 2):
                    wait(sp, out_half, 2 * s - 2)
                    sp.dma_start(out_tiles[s - 2], out_row[:]).then_inc(out_stored, 16)
                pair = 4 * (b + 1) + 2 * i + u
                if kind == "project" and not (isinstance(pair, int) and pair + 2 >= PAIRS):
                    sp.wait_ge(ctx_t, 2 * pair + 2)
                    load_pair(pair + 2, u)
                if not (isinstance(s, int) and s + 2 >= STEPS):
                    sp.wait_ge(x1_half, 2 * s + 2)
                    load_x(s + 2, u)

            run_steps(sp, step, straight=(4,))
            for s in (STEPS - 2, STEPS - 1):
                sp.wait_ge(out_half, 2 * s + 2)
                sp.dma_start(out_tiles[s], out_row[:]).then_inc(out_stored, 16)
            sp.wait_ge(out_stored, 16 * STEPS)

        @block.gpsimd
        def _(pool):
            pool.memset(ident[:], 0.0).then_inc(ident_zero, 1)
            pool.wait_ge(ident_zero, 1)
            pool.affine_select(out=ident[:], in_=ident[:], compare_op=ALU.not_equal, fill=1.0,
                               base=0, pattern=[[-1, P]], channel_multiplier=1) \
                .then_inc(ident_ready, 1)
            pool.memset(minus_half[:], -0.5).then_inc(consts_ready, 1)
            pool.memset(bound[:], 0.0).then_inc(consts_ready, 1)
            pool.iota(iota_i[:], pattern=[[1, EX]], base=0, channel_multiplier=0) \
                .then_inc(consts_ready, 1)
            pool.wait_ge(consts_ready, 3)
            pool.tensor_copy(iota[:], iota_i[:]).then_inc(consts_ready, 1)
            pool.wait_ge(tanh_ready, 1)
            pool.tensor_scalar(bias_row[:], bias_row[:], tanh_g[:, 1:2], 1.0, ALU.mult, ALU.mult) \
                .then_inc(bias_row_ready, 1)

            def rsqrt(k, n):
                _, _, var, rstd = ln[k]
                pool.wait_ge(ln_sem[k][2], n + 1)
                pool.tensor_tensor(rstd[:], var[:], minus_half[:], ALU.pow) \
                    .then_inc(ln_sem[k][3], 1)

            rsqrt("x", 0)
            pool.wait_ge(dve_bound, 1)
            pool.partition_all_reduce(bound_all[:], bound[:], P, RMAX).then_inc(bound_reduced, 1)
            pool.wait_ge(bias_row_ready, 1)

            def step(s, b, kind, i, u):
                if not (isinstance(s, int) and s + 1 >= STEPS):
                    rsqrt("x", s + 1)
                rsqrt("x1", s)
                pool.wait_ge(ln_sem["x1"][4], s + 1)
                pool.tensor_tensor(x1[u][:], x1[u][:], bias_row[:], ALU.add).then_inc(x1_biased, 1)

            run_steps(pool, step)

        @block.scalar
        def _(act):
            def hi_out(dst, h, ready, n, done, scale=1.0, src=None):
                act.wait_ge(ready, n)
                act.activation(dst, half(ps_t, h) if src is None else src, ACT.Copy, scale=scale) \
                    .then_inc(done, 1)

            def ctx_tile(f, v, u):
                cols = (2 * u + v) * P
                hi_out(ctxT[:, 0, :, cols:cols + P],
                       v, ctx_t, f + 1, ctx_hi,
                       src=half(ps_t, v).rearrange("p (k n) -> p k n", k=KC))

            def kq_out(g, i):
                cols = bass.ds(i * BANK, BANK)
                act.wait_ge(k_ready, g + 1)
                act.activation(kT[:, 0, cols], half(ps_score, 0), ACT.Identity, bias=bqk[:, 1:2]) \
                    .then_inc(k_hi, 1)
                act.wait_ge(q_ready, g + 1)
                act.activation(qT[:, cols], half(ps_score, 1), ACT.Identity, bias=bqk[:, 0:1]) \
                    .then_inc(q_copied, 1)

            def exp(j, v, ps):
                act.wait_ge(max_ready, j + 1)
                wait(act, probs_t, 2 * j - 2)
                act.activation(probs[v][:], ps[:], ACT.Exp, bias=neg_max[:, v:v + 1],
                               accum_out=row_sum[:, v:v + 1]).then_inc(exp_ready, 1)

            def normalise(j, v):
                act.wait_ge(inv_ready, j + 1)
                act.activation(probs[v][:], probs[v][:], ACT.Copy, scale=inv_sum[:, v:v + 1]) \
                    .then_inc(probs_ready, 1)

            def probs_out(j, par, col):
                for h in range(2):
                    hi_out(attnT[par][:, 0, HB * h:HB * h + HB, bass.ds(col * P, P)], h,
                           probs_t, 2 * j + h + 1, probs_hi, scale=PROB_SCALE,
                           src=half(ps_t, h).rearrange("p (k m) -> p k m", k=HB))

            def x_out(s):
                for h in range(2):
                    hi_out(xT[:, 0, HB * h:HB * h + HB, :], h, x_t, 2 * s + h + 1, x_hi)

            def prep(s, h):
                for (at_h, _), (n, job) in zip(PREP_AT[s], list(enumerate(PREP))[PREP_FIRST[s]:]):
                    if at_h == h:
                        dst, src, kind = prep_parts(n, 0)
                        act.wait_ge(prep_t, n + 1)
                        by = {"w": scale[:, 0:1], "a": scale[:, 1:2], "b": 1.0}[kind]
                        act.activation(dst, src, ACT.Copy, scale=by).then_inc(prep_hi, 1)

            act.wait_ge(small_loaded, 16 * 6)
            act.activation(tanh_g[:], g_in[:], ACT.Tanh).then_inc(tanh_ready, 1)
            for n in range(2):
                hi_out(wqkT[:, n, 0], n, wqk_t, n + 1, wqk_hi)
            for f in range(TILES):
                ctx_tile(f, f % 2, f // 2 % 2)
                if f % 4 == 3:
                    kq_out(f // 4, f // 4)
            exp(0, 0, ps_score)
            normalise(0, 0)
            exp(1, 1, ps_ffn)
            probs_out(0, 0, 0)
            normalise(1, 1)
            with act.Fori(1, TILES // 2) as i:
                for v, ps in ((0, ps_score), (1, ps_ffn)):
                    exp(2 * i + v, v, ps)
                    probs_out(2 * i + v - 1, 0, 2 * i + v - 1)
                    normalise(2 * i + v, v)
            probs_out(TILES - 1, 0, TILES - 1)
            x_out(0)
            act.wait_ge(w_loaded, 32)
            act.wait_ge(ab_loaded, 16 * 10)
            for n, (rows, src) in enumerate([(P, w_in[:, t, :]) for t in range(4)]
                                            + [(P, lora_a_in[:]), (EX, gate_in[0:EX, :])]):
                wait(act, act_bound, n)
                col = n if n < 4 else n + 1
                act.activation(ps_ffn[0:rows, :], src, ACT.Abs,
                               accum_out=bound_parts[0:rows, col:col + 1]).then_inc(act_bound, 1)

            def step(s, b, kind, i, u):
                if at_least(s, 1):
                    for h in range(2):
                        hi_out(x1T[:, 0, HB * h:HB * h + HB, :], h, x1_t, 2 * s - 1 + h, x1_hi)
                j = TILES * (b + 1) + 4 * i + 2 * u
                col = 4 * i + 2 * u
                if kind == "softmax":
                    exp(j, 0, ps_score)
                    normalise(j, 0)
                if isinstance(s, int) and s == 0:
                    act.wait_ge(scales_ready, 11)
                if isinstance(s, int) and s in PREP_AT:
                    prep(s, 0)
                if at_least(s, 1):
                    act.wait_ge(gap_ready, s)
                    act.activation(gap_exp[:], gap[:], ACT.Exp).then_inc(gap_exp_ready, 1)
                if isinstance(s, int) and s in PREP_AT:
                    prep(s, 1)
                if kind == "softmax":
                    probs_out(j, (b + 1) % 2, col)
                if kind == "project":
                    for v in range(2):
                        ctx_tile(j + v, v, u)
                if not (isinstance(s, int) and s + 1 >= STEPS):
                    x_out(s + 1)
                if at_least(s, 1):
                    hi_out(hT[:, 0, :], 1, h_t, s, h_hi, src=ps_ffn[:, BANK:BANK + ER])
                if kind == "softmax":
                    exp(j + 1, 1, ps_score)
                    normalise(j + 1, 1)
                    probs_out(j + 1, (b + 1) % 2, col + 1)
                if kind == "project" and u == 1:
                    kq_out(2 * (b + 1) + i, i)

            run_steps(act, step)
            for h in range(2):
                hi_out(x1T[:, 0, HB * h:HB * h + HB, :], h, x1_t, 2 * STEPS - 1 + h, x1_hi)
            act.wait_ge(gap_ready, STEPS)
            act.activation(gap_exp[:], gap[:], ACT.Exp).then_inc(gap_exp_ready, 1)
            hi_out(hT[:, 0, :], 1, h_t, STEPS, h_hi, src=ps_ffn[:, BANK:BANK + ER])

        @block.vector
        def _(dve):
            def lo_out(dst, hi, h, ready, n, done, scale=1.0, src=None):
                dve.wait_ge(ready, n)
                dve.scalar_tensor_tensor(out=dst, in0=half(ps_t, h) if src is None else src,
                                         scalar=scale, in1=hi, op0=ALU.mult, op1=ALU.subtract) \
                    .then_inc(done, 1)

            def ctx_tile(f, v, u):
                cols = (2 * u + v) * P
                lo_out(ctxT[:, 1, :, cols:cols + P], ctxT[:, 0, :, cols:cols + P].bitcast(F32),
                       v, ctx_hi, f + 1, ctx_lo,
                       src=half(ps_t, v).rearrange("p (k n) -> p k n", k=KC))

            def k_out(g, i):
                cols = bass.ds(i * BANK, BANK)
                dve.wait_ge(k_hi, g + 1)
                dve.scalar_tensor_tensor(out=kT[:, 1, cols], in0=half(ps_score, 0),
                                         scalar=bqk[:, 1:2], in1=kT[:, 0, cols].bitcast(F32),
                                         op0=ALU.add, op1=ALU.subtract).then_inc(k_lo, 1)

            def q_split(j, v, col):
                wait(dve, scores_ready, j - 1)
                src = qT[:, bass.ds(col * P, P)]
                dve.tensor_copy(q_tile[v][:, 0, :], src).then_inc(q_hi, 1)
                dve.wait_ge(q_hi, j + 1)
                dve.tensor_tensor(q_tile[v][:, 1, :], src, q_tile[v][:, 0, :].bitcast(F32),
                                  ALU.subtract).then_inc(q_lo, 1)

            def row_max(j, v, ps):
                dve.wait_ge(scores_ready, j + 1)
                dve.tensor_reduce(neg_max[:, v:v + 1], ps[:], AX.X, ALU.max, negate=True) \
                    .then_inc(max_ready, 1)

            def inv_row_sum(j, v):
                dve.wait_ge(exp_ready, j + 1)
                dve.reciprocal(inv_sum[:, v:v + 1], row_sum[:, v:v + 1]).then_inc(inv_ready, 1)

            def probs_out(j, par, col):
                for h in range(2):
                    ks = slice(HB * h, HB * h + HB)
                    lo_out(attnT[par][:, 1, ks, bass.ds(col * P, P)],
                           attnT[par][:, 0, ks, bass.ds(col * P, P)], h,
                           probs_hi, 2 * j + h + 1, probs_lo, scale=PROB_SCALE,
                           src=half(ps_t, h).rearrange("p (k m) -> p k m", k=HB))

            def ln_bn(k, src, h):
                dve.bn_stats(ln[k][0][:, 6 * h:6 * h + 6], half(src, h)).then_inc(ln_sem[k][0], 1)

            def ln_var(k, n):
                bn, mv, var, _ = ln[k]
                dve.wait_ge(ln_sem[k][0], 2 * n + 2)
                dve.memset(wait_word[:], 0.0)
                dve.bn_aggr(mv[:], bn[:]).then_inc(ln_sem[k][1], 1)
                dve.wait_ge(ln_sem[k][1], n + 1)
                dve.tensor_scalar(var[:], mv[:, 1:2], EPS, NORM_SCALE ** -2, ALU.add, ALU.mult) \
                    .then_inc(ln_sem[k][2], 1)

            def ln_norm(k, n, dst, src, used):
                _, mv, _, rstd = ln[k]
                dve.wait_ge(ln_sem[k][3], n + 1)
                wait(dve, used, 2 * n)
                dve.tensor_scalar(dst[:], src[:], mv[:, 0:1], rstd[:], ALU.subtract, ALU.mult) \
                    .then_inc(ln_sem[k][4], 1)

            def x_stats(s, u):
                dve.wait_ge(x_loaded[u], 16 * load_count(s))
                for h in range(2):
                    ln_bn("x", x_in[u], h)
                ln_var("x", s)

            def load_count(s):
                return s // 2 + 1

            def x_out(s):
                for h in range(2):
                    ks = slice(HB * h, HB * h + HB)
                    lo_out(xT[:, 1, ks, :], xT[:, 0, ks, :], h, x_hi, 2 * s + h + 1, x_lo,
                           src=half(ps_t, h).rearrange("p (k l) -> p k l", k=HB))

            def x1_out(s):
                for h in range(2):
                    ks = slice(HB * h, HB * h + HB)
                    lo_out(x1T[:, 1, ks, :], x1T[:, 0, ks, :], h, x1_hi, 2 * s + h + 1, x1_lo,
                           src=half(ps_t, h).rearrange("p (k l) -> p k l", k=HB))

            def residual(s, u, h):
                dve.wait_ge(attn_ready, 2 * s + h + 1)
                wait(dve, out_half, 2 * s - 4 + 2)
                dve.scalar_tensor_tensor(out=half(x1[u], h), in0=half(ps_attn, h),
                                         scalar=attn_coef[:], in1=half(x_in[u], h),
                                         op0=ALU.mult, op1=ALU.add).then_inc(x1_half, 1)
                dve.wait_ge(x1_half, 2 * s + h + 1)
                ln_bn("x1", x1[u], h)

            def finish(s, u):
                dve.wait_ge(x1_biased, s + 1)
                wait(dve, out_stored, 16 * s)
                for h in range(2):
                    dve.wait_ge(ffn_ready, 2 * s + h + 1)
                    dve.scalar_tensor_tensor(out=half(out_row, h), in0=half(ps_ffn, h),
                                             scalar=ffn_coef[:], in1=half(x1[u], h),
                                             op0=ALU.mult, op1=ALU.add).then_inc(out_half, 1)

            def gates(s):
                def link(ins):
                    ins.then_inc(gate_chain, 1)

                def linked(n):
                    dve.wait_ge(gate_chain, GATE_LINKS * s + n)

                dve.wait_ge(ga_ready, s + 1)
                dve.tensor_copy(ga[:], ps_ffn[:, BANK:BANK + ER + EX]).then_inc(ga_copied, 1)
                dve.wait_ge(ga_copied, s + 1)
                link(dve.scalar_tensor_tensor(out=logits[:], in0=ga[:, ER:ER + EX],
                                              scalar=logit_coef[:], in1=gate_bias[:],
                                              op0=ALU.mult, op1=ALU.add))
                linked(1)
                dve.memset(wait_word[:], 0.0)
                link(dve.max(top[:], logits[:]))
                linked(2)
                dve.tensor_tensor(gap[:], top[:, 1:2], top[:, 0:1], ALU.subtract) \
                    .then_inc(gap_ready, 1)
                link(dve.max_index(top_idx[:], top[:], logits[:]))
                linked(3)
                link(dve.tensor_copy(top_idx_f[:], top_idx[:, 0:2]))
                dve.wait_ge(gap_exp_ready, s + 1)
                link(dve.tensor_scalar(gate_den[:], gap_exp[:], 1.0, None, ALU.add))
                linked(5)
                link(dve.reciprocal(gate_inv[:], gate_den[:]))
                linked(6)
                link(dve.tensor_scalar(gate_top[:, 0:1], gate_inv[:], lora_coef[:], None, ALU.mult))
                linked(7)
                link(dve.tensor_tensor(gate_top[:, 1:2], gate_top[:, 0:1], gap_exp[:], ALU.mult))
                link(dve.tensor_scalar(gate_of[:, 0, :], iota[:], top_idx_f[:, 0:1],
                                       gate_top[:, 0:1], ALU.is_equal, ALU.mult))
                linked(8)
                link(dve.tensor_scalar(gate_of[:, 1, :], iota[:], top_idx_f[:, 1:2],
                                       gate_top[:, 1:2], ALU.is_equal, ALU.mult))
                linked(10)
                link(dve.tensor_tensor(gate_of[:, 2, :], gate_of[:, 0, :], gate_of[:, 1, :],
                                       ALU.add))
                linked(11)
                wait(dve, h_t, s)
                dve.tensor_tensor(h_row[:].rearrange("p (e r) -> p e r", e=EX),
                                  ga[:, 0:ER].rearrange("p (e r) -> p e r", e=EX),
                                  gate_of[:, 2, :].unsqueeze(2).to_broadcast([P, EX, R]),
                                  ALU.mult).then_inc(h_ready, 1)

            def h_out(s):
                lo_out(hT[:, 1, :], hT[:, 0, :].bitcast(F32), 1, h_hi, s + 1, h_lo,
                       src=ps_ffn[:, BANK:BANK + ER])

            def prep(s, h):
                for (at_h, _), (n, job) in zip(PREP_AT[s], list(enumerate(PREP))[PREP_FIRST[s]:]):
                    if at_h == h:
                        dst, src, kind = prep_parts(n, 1)
                        hi = prep_parts(n, 0)[0]
                        by = {"w": scale[:, 0:1], "a": scale[:, 1:2], "b": 1.0}[kind]
                        lo_out(dst, hi.bitcast(F32) if kind == "b" else hi, n % 2,
                               prep_hi, n + 1, prep_lo, scale=by, src=src)

            def weight_scales():
                dve.wait_ge(w_loaded, 32)
                dve.tensor_reduce(bound_parts[:, 4:5], w_in[:, 4:8, :], AX.XY, ALU.max,
                                  apply_absolute_value=True).then_inc(scales_ready, 1)
                dve.wait_ge(act_bound, 6)
                dve.wait_ge(scales_ready, 1)
                dve.wait_ge(consts_ready, 4)
                dve.tensor_reduce(bound[:, 0:1], bound_parts[:, 0:5], AX.X, ALU.max) \
                    .then_inc(scales_ready, 1)
                dve.tensor_copy(bound[:, 1:2], bound_parts[:, 5:6]).then_inc(scales_ready, 1)
                dve.wait_ge(scales_ready, 3)
                dve.tensor_tensor(bound[0:EX, 1:2], bound_parts[0:EX, 5:6], bound_parts[0:EX, 6:7],
                                  ALU.max).then_inc(dve_bound, 1)
                dve.wait_ge(bound_reduced, 1)
                dve.tensor_scalar(bound_low[:], bound_all[:], 2.0 ** -60, None, ALU.max) \
                    .then_inc(scales_ready, 1)
                dve.wait_ge(scales_ready, 4)
                dve.tensor_scalar(pow2[:].bitcast(U32), bound_low[:].bitcast(U32), EXPONENT, None,
                                  ALU.bitwise_and).then_inc(scales_ready, 1)
                dve.wait_ge(scales_ready, 5)
                dve.reciprocal(inv_pow2[:], pow2[:]).then_inc(scales_ready, 1)
                dve.wait_ge(scales_ready, 6)
                dve.wait_ge(tanh_ready, 1)
                dve.tensor_scalar(attn_coef[:], tanh_g[:, 0:1], 1.0 / (NORM_SCALE * PROB_SCALE),
                                  None, ALU.mult).then_inc(scales_ready, 1)
                dve.tensor_scalar(ffn_coef[:], pow2[:, 0:1], tanh_g[:, 1:2],
                                  1.0 / (NORM_SCALE * W_TOP), ALU.mult, ALU.mult) \
                    .then_inc(scales_ready, 1)
                dve.tensor_scalar(logit_coef[:], pow2[:, 1:2], 1.0 / (NORM_SCALE * W_TOP), None,
                                  ALU.mult).then_inc(scales_ready, 1)
                dve.tensor_scalar(lora_coef[:], pow2[:, 1:2], inv_pow2[:, 0:1], None, ALU.mult) \
                    .then_inc(scales_ready, 1)
                dve.tensor_scalar(scale[:], inv_pow2[:], W_TOP, None, ALU.mult) \
                    .then_inc(scales_ready, 1)
                dve.wait_ge(scales_ready, 11)

            for n in range(2):
                lo_out(wqkT[:, n, 1], wqkT[:, n, 0].bitcast(F32), n, wqk_hi, n + 1, wqk_lo,
                       src=half(ps_t, n).rearrange("p (k d) -> p k d", k=KC))
            dve.wait_ge(small_loaded, 16 * 6)
            for f in range(TILES):
                ctx_tile(f, f % 2, f // 2 % 2)
                if f == 1:
                    x_stats(0, 0)
                if f % 4 == 3:
                    k_out(f // 4, f // 4)
            ln_norm("x", 0, x_norm, x_in[0], x_t)
            dve.wait_ge(q_copied, 2)
            for j, ps in ((0, ps_score), (1, ps_ffn)):
                q_split(j, j, j)
            row_max(0, 0, ps_score)
            inv_row_sum(0, 0)
            row_max(1, 1, ps_ffn)
            inv_row_sum(1, 1)
            with dve.Fori(1, TILES // 2) as i:
                for v, ps in ((0, ps_score), (1, ps_ffn)):
                    q_split(2 * i + v, v, 2 * i + v)
                    row_max(2 * i + v, v, ps)
                    probs_out(2 * i + v - 2, 0, 2 * i + v - 2)
                    inv_row_sum(2 * i + v, v)
            for j in (TILES - 2, TILES - 1):
                probs_out(j, 0, j)
            x_out(0)

            def step(s, b, kind, i, u):
                j = TILES * (b + 1) + 4 * i + 2 * u
                col = 4 * i + 2 * u
                if kind == "softmax":
                    if u == 0:
                        dve.wait_ge(q_copied, 2 * (b + 2))
                    q_split(j, 0, col)
                if isinstance(s, int) and s == 0:
                    weight_scales()
                if at_least(s, 1):
                    x1_out(s - 1)
                if at_least(s, 2):
                    finish(s - 2, u)
                more = not (isinstance(s, int) and s + 1 >= STEPS)
                if more:
                    x_stats_next(s, i, u, b)
                if kind == "softmax":
                    row_max(j, 0, ps_score)
                if isinstance(s, int) and s in PREP_AT:
                    prep(s, 0)
                if more:
                    ln_norm("x", s + 1, x_norm, x_in[1 - u], x_t)
                residual(s, u, 0)
                if kind == "softmax":
                    inv_row_sum(j, 0)
                    q_split(j + 1, 1, col + 1)
                if at_least(s, 1):
                    gates(s - 1)
                if isinstance(s, int) and s in PREP_AT:
                    prep(s, 1)
                if kind == "softmax":
                    probs_out(j, (b + 1) % 2, col)
                if kind == "project":
                    for v in range(2):
                        ctx_tile(j + v, v, u)
                residual(s, u, 1)
                ln_var("x1", s)
                if more:
                    x_out(s + 1)
                ln_norm("x1", s, x1_norm, x1[u], x1_t)
                if at_least(s, 1):
                    h_out(s - 1)
                if kind == "softmax":
                    row_max(j + 1, 1, ps_score)
                    inv_row_sum(j + 1, 1)
                    probs_out(j + 1, (b + 1) % 2, col + 1)
                if kind == "project" and u == 1:
                    k_out(2 * (b + 1) + i, i)

            def x_stats_next(s, i, u, b):
                pairs = (s - u) * 8 + 16 * (1 + u)
                dve.wait_ge(x_loaded[1 - u], pairs)
                for h in range(2):
                    ln_bn("x", x_in[1 - u], h)
                ln_var("x", s + 1)

            run_steps(dve, step)
            x1_out(STEPS - 1)
            finish(STEPS - 2, 0)
            gates(STEPS - 1)
            h_out(STEPS - 1)
            finish(STEPS - 1, 1)

        @block.tensor
        def _(pe):
            PASSES = ((0, 0), (0, 1), (1, 0))

            def product(ps, lhs, rhs, k, first, last):
                for n, (a, c) in enumerate(PASSES):
                    mm = pe.matmul(ps, lhs(a), rhs(c), start=first and n == 0,
                                   stop=last and n == len(PASSES) - 1)
                return mm

            def transposes(h, blocks):
                for n, src in enumerate(blocks):
                    mm = pe.transpose(ps_t[:, h * BANK + n * P:h * BANK + (n + 1) * P], src, ident[:])
                return mm

            def attend(h, par, k):
                return product(half(ps_attn, h), lambda a: xT[:, a, k, :],
                               lambda c: attnT[par][:, c, k, h * BANK:(h + 1) * BANK],
                               k, k == 0, k == KD - 1)

            def linear(h, k):
                return product(half(ps_ffn, h), lambda a: x1T[:, a, k, :],
                               lambda c: wT[:, c, k, h * BANK:(h + 1) * BANK], k, k == 0, False)

            def gate_products(s):
                pe.wait_ge(x1_lo, 2 * s + 2)
                wait(pe, out_half, 2 * s)
                for k in range(KD):
                    mm = product(ps_ffn[:, BANK:BANK + ER + EX], lambda a: x1T[:, a, k, :],
                                 lambda c: agT[:, c, k, :], k, k == 0, k == KD - 1)
                mm.then_inc(ga_ready, 1)

            def gated_transpose(s):
                pe.wait_ge(h_ready, s + 1)
                pe.transpose(ps_ffn[:, BANK:BANK + ER], h_row[:], ident[:]).then_inc(h_t, 1)

            def lora(s):
                for h in range(2):
                    product(half(ps_ffn, h), lambda a: hT[:, a, :],
                            lambda c: bT[:, c, h * BANK:(h + 1) * BANK], 0, False, True) \
                        .then_inc(ffn_ready, 1)

            def scores(j, v, ps):
                pe.wait_ge(q_lo, j + 1)
                for h in range(2):
                    mm = product(half(ps, h), lambda a: q_tile[v][:, a, :],
                                 lambda c: kT[:, c, h * BANK:(h + 1) * BANK], 0, True, True)
                mm.then_inc(scores_ready, 1)

            def probs_transpose(j, v, free):
                pe.wait_ge(probs_ready, j + 1)
                for h in range(2):
                    free(h)
                    transposes(h, [probs[v][:, (HB * h + n) * P:(HB * h + n + 1) * P]
                                   for n in range(HB)]).then_inc(probs_t, 1)

            def rows_transpose(src, ready, count, done, free):
                pe.wait_ge(ready, count)
                for h in range(2):
                    free(h)
                    transposes(h, [src[:, (HB * h + n) * P:(HB * h + n + 1) * P]
                                   for n in range(HB)]).then_inc(done, 1)

            def ctx_transpose(pair, loads, u, free):
                pe.wait_ge(ctx_loaded[u], 16 * loads)
                for v in range(2):
                    free(v)
                    transposes(v, [ctx_in[u][:, v, n * P:(n + 1) * P] for n in range(KC)]) \
                        .then_inc(ctx_t, 1)

            def project(g):
                pe.wait_ge(ctx_lo, 4 * g + 4)
                for n, done in ((1, k_ready), (0, q_ready)):
                    for k in range(KC):
                        mm = product(half(ps_score, 1 - n), lambda a: wqkT[:, n, a, k, :],
                                     lambda c: ctxT[:, c, k, :], k, k == 0, k == KC - 1)
                    mm.then_inc(done, 1)

            def prep_job(n, free):
                name, at = PREP[n]
                free()
                if name == "lora_b":
                    mm = transposes(n % 2, [lora_b_in[:, HB * at + t].rearrange("p e r -> p (e r)")
                                            for t in range(HB)])
                elif name == "lora_a":
                    mm = transposes(n % 2, [lora_a_in[:, (HB * at + k) * P:(HB * at + k + 1) * P]
                                            for k in range(HB)])
                elif name == "gate":
                    for k in range(KD):
                        at = n % 2 * BANK + k * EX
                        mm = pe.transpose(ps_t[:, at:at + EX], gate_in[0:EX, k * P:(k + 1) * P],
                                          ident[0:EX, 0:EX])
                else:
                    tile, h = at // 2, at % 2
                    mm = transposes(n % 2, [w_in[:, tile, (HB * h + k) * P:(HB * h + k + 1) * P]
                                            for k in range(HB)])
                mm.then_inc(prep_t, 1)

            pe.wait_ge(ident_ready, 1)
            pe.wait_ge(wqk_loaded, 32)
            for n in range(2):
                transposes(n, [wqk_in[:, n, k * P:(k + 1) * P] for k in range(KC)]) \
                    .then_inc(wqk_t, 1)
            pe.wait_ge(wqk_lo, 2)
            for pair in range(4):
                ctx_transpose(pair, pair // 2 + 1, pair % 2,
                              lambda v: wait(pe, ctx_lo, 2 * pair - 1 + v))
                if pair % 2:
                    wait(pe, k_lo, pair // 2)
                    wait(pe, q_copied, pair // 2)
                    project(pair // 2)
            pe.wait_ge(k_lo, 2)
            pe.wait_ge(q_copied, 2)
            scores(0, 0, ps_score)
            scores(1, 1, ps_ffn)
            probs_transpose(0, 0, lambda h: pe.wait_ge(ctx_lo, TILES - 1 + h))
            with pe.Fori(1, TILES // 2) as i:
                for v, ps in ((0, ps_score), (1, ps_ffn)):
                    pe.wait_ge(exp_ready, 2 * i + v - 1)
                    scores(2 * i + v, v, ps)
                    probs_transpose(2 * i + v - 1, 1 - v,
                                    lambda h: pe.wait_ge(probs_lo, 4 * i + 2 * v - 3 + h))
            probs_transpose(TILES - 1, 1, lambda h: pe.wait_ge(probs_lo, 2 * TILES - 3 + h))
            rows_transpose(x_norm, ln_sem["x"][4], 1, x_t,
                           lambda h: pe.wait_ge(probs_lo, 2 * TILES - 1 + h))

            def step(s, b, kind, i, u):
                preparing = isinstance(s, int) and s in PREP_AT
                j = TILES * (b + 1) + 4 * i + 2 * u
                par = b % 2

                def attend_half(h, between=None):
                    for k in range(KD):
                        mm = attend(h, par, k)
                        if k == KD - 1:
                            mm.then_inc(attn_ready, 1)
                        if k == KD // 2 - 1 and between:
                            between()
                        if preparing and (h, k) in PREP_AT[s]:
                            n = PREP_FIRST[s] + PREP_AT[s].index((h, k))
                            prep_job(n, lambda: prep_free(n))

                def prep_free(n):
                    if n == 0:
                        pe.wait_ge(ab_loaded, 16 * 10)
                        pe.wait_ge(x_lo, 2)
                        pe.wait_ge(w_loaded, 32)
                    elif n >= 2:
                        pe.wait_ge(prep_lo, n - 1)
                    if n == PREP_FIRST[1]:
                        pe.wait_ge(x1_lo, 2)

                def first_job():
                    if kind == "softmax":
                        if u == 0:
                            pe.wait_ge(k_lo, 2 * (b + 2))
                            pe.wait_ge(q_copied, 2 * (b + 2))
                        pe.wait_ge(exp_ready, j)
                        scores(j, 0, ps_score)

                pe.wait_ge(x_lo, 2 * s + 2)
                if u == 0:
                    pe.wait_ge(probs_lo, 2 * TILES * (b + 1))
                wait(pe, x1_half, 2 * s - 1)
                attend_half(0, first_job)
                if at_least(s, 1):
                    if isinstance(s, int) and s == 1:
                        pe.wait_ge(prep_lo, 5)
                    gate_products(s - 1)
                wait(pe, x1_half, 2 * s)

                def second_job():
                    if kind == "softmax":
                        probs_transpose(j, 0, lambda h: pe.wait_ge(x1_lo, 2 * s - 1 + h))
                    if kind == "project" and not preparing:
                        ctx_transpose(None, 2 * (b + 1) + i + 1, u,
                                      lambda v: pe.wait_ge(x1_lo, 2 * s - 1 + v))

                attend_half(1, second_job)
                if preparing:
                    n = PREP_FIRST[s] + len(PREP_AT[s])
                    ctx_transpose(None, 2 * (b + 1) + i + 1, u,
                                  lambda v: pe.wait_ge(prep_lo, n))

                def after_job(h):
                    if kind == "softmax":
                        pe.wait_ge(probs_lo, 2 * j + h + 1)
                    elif kind == "project":
                        pe.wait_ge(ctx_lo, j + h + 1)
                    else:
                        pe.wait_ge(x1_lo, 2 * s - 1 + h)

                more = not (isinstance(s, int) and s + 1 >= STEPS)
                if more:
                    rows_transpose(x_norm, ln_sem["x"][4], s + 2, x_t, after_job)
                linear_first, linear_rest = range(KD // 2), range(KD // 2, KD)
                if at_least(s, 1):
                    if isinstance(s, int) and s == 1:
                        pe.wait_ge(prep_lo, len(PREP))
                    wait(pe, out_half, 2 * s - 3)
                    for k in linear_first:
                        linear(0, k)
                    gated_transpose(s - 1)
                if kind == "softmax":
                    pe.wait_ge(exp_ready, j + 1)
                    scores(j + 1, 1, ps_score)
                if kind == "project" and u == 1:
                    wait(pe, exp_ready, TILES * (b + 1))
                    if not (isinstance(i, int) and i == 0):
                        pe.wait_ge(k_lo, 2 * (b + 1) + i)
                        pe.wait_ge(q_copied, 2 * (b + 1) + i)
                    project(2 * (b + 1) + i)
                if at_least(s, 1):
                    for k in linear_rest:
                        linear(0, k)
                    pe.wait_ge(h_lo, s)
                    for k in linear_first:
                        linear(1, k)
                if kind == "softmax":
                    probs_transpose(j + 1, 1, lambda h: pe.wait_ge(x_lo, 2 * s + 3 + h))
                if at_least(s, 1):
                    for k in linear_rest:
                        linear(1, k)
                    lora(s - 1)

                def before_x1(h):
                    if kind == "softmax":
                        pe.wait_ge(probs_lo, 2 * j + h + 3)
                    elif more:
                        pe.wait_ge(x_lo, 2 * s + 3 + h)

                rows_transpose(x1_norm, ln_sem["x1"][4], s + 1, x1_t, before_x1)

            run_steps(pe, step)
            gate_products(STEPS - 1)
            pe.wait_ge(out_half, 2 * STEPS - 3)
            for k in range(KD):
                linear(0, k)
            gated_transpose(STEPS - 1)
            pe.wait_ge(h_lo, STEPS)
            for k in range(KD):
                linear(1, k)
            lora(STEPS - 1)


_INS = ["x", "ctx_1024", "g_xattn", "g_ffn", "L0_xattn_Wq", "L0_xattn_bq", "L0_xattn_Wk",
        "L0_xattn_bk", "L0_ffn_W", "L0_ffn_b", "L0_ffn_lora_A", "L0_ffn_lora_B", "L0_ffn_gate_w",
        "L0_ffn_gate_b"]
_OUTS = [((B, L, D), "float32")]


def kernel(**inputs):
    import numpy as _np
    import concourse.bacc as _bacc
    from concourse import mybir as _mybir
    from concourse.bass_utils import run_bass_kernel_spmd as _run

    nc = _bacc.Bacc("TRN2", target_bir_lowering=False, num_devices=1)
    arrays, args = {}, []
    for name in _INS:
        a = _np.ascontiguousarray(inputs[name])
        arrays[f"in_{name}_dram"] = a
        args.append(nc.dram_tensor(f"in_{name}_dram", a.shape, _mybir.dt.from_np(a.dtype),
                                   kind="ExternalInput").ap())
    for i, (shape, dtype) in enumerate(_OUTS):
        dt = _mybir.dt.from_np(_np.dtype(dtype))
        args.append(nc.dram_tensor(f"out_{i}_dram", shape, dt, kind="ExternalOutput").ap())
    flamingo_block(nc, *args)
    r = _run(nc, [arrays], core_ids=[0])
    return r.results[0]["out_0_dram"]
```

```python
from contextlib import ExitStack

import concourse.bass as bass
from concourse import mybir

F32 = mybir.dt.float32
F32R = mybir.dt.float32r
F16 = mybir.dt.float16
U32 = mybir.dt.uint32
I32 = mybir.dt.int32
ALU = mybir.AluOpType
ACT = mybir.ActivationFunctionType
AX = mybir.AxisListType
RMAX = bass.bass_isa.ReduceOp.max

P = 128
BANK = 512
B, L, D = 4, 1024, 1024
N, C, DH = 1024, 512, 128
EX, R = 8, 16
ER = EX * R
EPS = 1e-5

TILES = L // P
STEPS = B * TILES
KD = D // P
KC = C // P
HB = BANK // P

NORM_SCALE = 2.0 ** 10
PROB_SCALE = 2.0 ** 15
W_TOP = 2.0 ** 14
EXPONENT = 0x7F800000
GATE_LINKS = 11

SEGMENTS = [(0, 0, 2, "project", False), (0, 4, 2, "softmax", True),
            (1, 0, 2, "project", True), (1, 4, 2, "softmax", True),
            (2, 0, 2, "project", True), (2, 4, 2, "softmax", True),
            (3, 0, 3, None, True), (3, 6, 1, None, False)]

PREP = ([("lora_b", 0), ("lora_b", 1), ("lora_a", 0), ("lora_a", 1), ("gate", 0)]
        + [("w", n) for n in range(2 * TILES)])
PREP_AT = {0: [(h, k) for h in range(2) for k in range(KD)], 1: [(0, k) for k in range(5)]}
PREP_FIRST = {0: 0, 1: len(PREP_AT[0])}


def run_steps(eng, step, straight=()):
    for n, (b, first, pairs, kind, looped) in enumerate(SEGMENTS):
        base = TILES * b + first
        if looped and n not in straight:
            with eng.Fori(0, pairs) as i:
                for u in range(2):
                    step(base + 2 * i + u, b, kind, i, u)
        else:
            for i in range(pairs):
                for u in range(2):
                    step(base + 2 * i + u, b, kind, i, u)


def wait(eng, sem, value):
    if isinstance(value, int) and value <= 0:
        return
    eng.wait_ge(sem, value)


def at_least(s, n):
    return not isinstance(s, int) or s >= n


def has_next(s):
    return not (isinstance(s, int) and s + 1 >= STEPS)


def flamingo_block(nc, x, ctx_tokens, g_xattn, g_ffn, Wq, bq, Wk, bk, W, bias, lora_A, lora_B,
                   gate_w, gate_b, out):
    x_tiles = x.rearrange("b (t p) d -> (b t) p d", p=P)
    out_tiles = out.rearrange("b (t p) d -> (b t) p d", p=P)
    ctx_pairs = ctx_tokens.rearrange("b (q t p) c -> (b q) p t c", p=P, t=2)
    PAIRS = B * N // (2 * P)

    with ExitStack() as stack:
        def sb(name, shape, dt):
            return stack.enter_context(nc.sbuf_tensor(name, shape, dt))

        def sem(name):
            return stack.enter_context(nc.semaphore(name))

        attnT = [sb(f"attnT{v}", [P, 2, KD, L], F16) for v in range(2)]
        wT = sb("wT", [P, 2, KD, D], F16)
        agT = sb("agT", [P, 2, KD, ER + EX], F16)
        bT = sb("bT", [P, 2, D], F32R)
        xT = sb("xT", [P, 2, KD, P], F16)
        x1T = [sb(f"x1T{u}", [P, 2, KD, P], F16) for u in range(2)]
        ctxT = sb("ctxT", [P, 2, KC, BANK], F32R)
        wqkT = sb("wqkT", [P, 2, 2, KC, DH], F32R)
        kT = sb("kT", [P, 2, N], F32R)
        qT = sb("qT", [P, L], F32)
        q_tile = [sb(f"q_tile{v}", [P, 2, P], F32R) for v in range(2)]
        hT = sb("hT", [P, 2, P], F32R)
        ctx_in = sb("ctx_in", [P, 2, C], F32)
        x_in = [sb(f"x_in{u}", [P, D], F32) for u in range(2)]
        x1 = [sb(f"x1_{u}", [P, D], F32) for u in range(2)]
        row_norm = sb("row_norm", [P, D], F32)
        row_split = sb("row_split", [P, 2, D], F16)
        out_row = sb("out_row", [P, D], F32)
        exp_row = sb("exp_row", [P, N], F32)
        probs_split = sb("probs_split", [P, 2, N], F16)
        bias_row = sb("bias_row", [P, D], F32)
        ident = sb("ident", [P, P], F32)
        bqk = sb("bqk", [P, 2], F32)
        g_in = sb("g_in", [P, 2], F32)
        tanh_g = sb("tanh_g", [P, 2], F32)
        bound_parts = sb("bound_parts", [P, 10], F32)
        bound = sb("bound", [P, 2], F32)
        bound_all = sb("bound_all", [P, 2], F32)
        bound_low = sb("bound_low", [P, 2], F32)
        pow2 = sb("pow2", [P, 2], F32)
        inv_pow2 = sb("inv_pow2", [P, 2], F32)
        scale = sb("scale", [P, 2], F32)
        attn_coef = sb("attn_coef", [P, 1], F32)
        ffn_coef = sb("ffn_coef", [P, 1], F32)
        logit_coef = sb("logit_coef", [P, 1], F32)
        lora_coef = sb("lora_coef", [P, 1], F32)
        gate_bias = sb("gate_bias", [P, EX], F32)
        iota_i = sb("iota_i", [P, EX], I32)
        iota = sb("iota", [P, EX], F32)
        minus_half = sb("minus_half", [P, 1], F32)
        neg_max = sb("neg_max", [P, 2], F32)
        row_sum = sb("row_sum", [P, 2], F32)
        sum_scaled = sb("sum_scaled", [P, 2], F32)
        inv_sum = sb("inv_sum", [P, 2], F32)
        ln = {k: (sb(f"{k}_bn", [P, 12], F32), sb(f"{k}_mv", [P, 2], F32),
                  sb(f"{k}_var", [P, 1], F32), sb(f"{k}_rstd", [P, 1], F32)) for k in ("x", "x1")}
        ga = sb("ga", [P, ER + EX], F32)
        logits = sb("logits", [P, EX], F32)
        top = sb("top", [P, 8], F32)
        top_idx = sb("top_idx", [P, 8], U32)
        top_idx_f = sb("top_idx_f", [P, 2], F32)
        wait_word = sb("wait_word", [P, 1], F32)
        gap = sb("gap", [P, 1], F32)
        gap_exp = sb("gap_exp", [P, 1], F32)
        gate_den = sb("gate_den", [P, 1], F32)
        gate_inv = sb("gate_inv", [P, 1], F32)
        gate_top = sb("gate_top", [P, 2], F32)
        gate_of = sb("gate_of", [P, 3, EX], F32)
        h_row = sb("h_row", [P, ER], F32)

        w_in = attnT[1][:].rearrange("p a k m -> p (a k m)").bitcast(F32) \
            .rearrange("p (t m) -> p t m", t=TILES)
        wqk_in = x1[0][:].rearrange("p (a c) -> p a c", a=2)
        lora_b_in = x1[0][:].rearrange("p (t e r) -> p t e r", t=TILES, e=EX)
        lora_a_in = x1[1]
        gate_in = x1T[0][:].rearrange("p a k l -> p (a k l)").bitcast(F32)
        first_ctx = [ctx_in[:]] + [t.rearrange("p (t c) -> p t c", t=2) for t in (
            exp_row[:], out_row[:],
            probs_split[:].rearrange("p a n -> p (a n)").bitcast(F32))]
        exp_rows = [exp_row[:], out_row[:]]
        probs_splits = [probs_split[:], x1T[1][:].rearrange("p a k l -> p a (k l)")]

        ps_attn = stack.enter_context(nc.psum_tensor("ps_attn", [P, 2 * BANK], F32))
        ps_ffn = stack.enter_context(nc.psum_tensor("ps_ffn", [P, 2 * BANK], F32))
        ps_score = stack.enter_context(nc.psum_tensor("ps_score", [P, 2 * BANK], F32))
        ps_t = stack.enter_context(nc.psum_tensor("ps_t", [P, 2 * BANK], F32))

        def half(ps, h):
            return ps[:, h * BANK:(h + 1) * BANK]

        def first_ps(f):
            return half((ps_t, ps_t, ps_ffn, ps_ffn)[f % 4], f % 2)

        def prep_parts(n, part):
            name, at = PREP[n]
            ps = half(ps_t, n % 2)
            if name == "lora_b":
                return bT[:, part, at * BANK:(at + 1) * BANK], ps, 1.0
            if name == "lora_a":
                return (agT[:, part, HB * at:HB * at + HB, 0:ER],
                        ps.rearrange("p (k n) -> p k n", k=HB), scale[:, 1:2])
            if name == "gate":
                return (agT[:, part, :, ER:ER + EX],
                        ps[:, 0:KD * EX].rearrange("p (k n) -> p k n", k=KD), scale[:, 1:2])
            tile, h = at // 2, at % 2
            return (wT[:, part, HB * h:HB * h + HB, tile * P:(tile + 1) * P],
                    ps.rearrange("p (k n) -> p k n", k=HB), scale[:, 0:1])

        wqk_loaded, ab_loaded, small_loaded, bias_loaded = map(sem, (
            "wqk_loaded", "ab_loaded", "small_loaded", "bias_loaded"))
        w_loaded = [sem(f"w_loaded{n}") for n in range(TILES // 2)]
        first_ctx_loaded = [sem(f"first_ctx_loaded{n}") for n in range(4)]
        ctx_loaded, lora_b_loaded = sem("ctx_loaded"), sem("lora_b_loaded")
        x_loaded = [sem(f"x_loaded{u}") for u in range(2)]
        out_stored = sem("out_stored")
        consts_ready, ident_zero, ident_ready, bias_row_ready = map(sem, (
            "consts_ready", "ident_zero", "ident_ready", "bias_row_ready"))
        tanh_ready, act_bound, dve_bound, bound_reduced, scales_ready = map(sem, (
            "tanh_ready", "act_bound", "dve_bound", "bound_reduced", "scales_ready"))
        wqk_t, wqk_hi, wqk_lo = map(sem, ("wqk_t", "wqk_hi", "wqk_lo"))
        prep_t, prep_hi, prep_lo = map(sem, ("prep_t", "prep_hi", "prep_lo"))
        ctx_t, ctx_hi, ctx_lo = map(sem, ("ctx_t", "ctx_hi", "ctx_lo"))
        k_ready, q_ready, k_hi, k_lo, q_copied = map(sem, (
            "k_ready", "q_ready", "k_hi", "k_lo", "q_copied"))
        q_hi, q_lo, scores_ready, max_ready, exp_ready, sum_ready, inv_ready = map(sem, (
            "q_hi", "q_lo", "scores_ready", "max_ready", "exp_ready", "sum_ready", "inv_ready"))
        probs_hi, probs_lo = sem("probs_hi"), sem("probs_lo")
        probs_t = [sem(f"probs_t{v}") for v in range(2)]
        x_hi, x_lo, x_t = map(sem, ("x_hi", "x_lo", "x_t"))
        x1_hi, x1_lo, x1_t = map(sem, ("x1_hi", "x1_lo", "x1_t"))
        attn_ready, x1_half, ffn_ready, out_half = map(sem, (
            "attn_ready", "x1_half", "ffn_ready", "out_half"))
        ln_sem = {k: [sem(f"{k}_{w}") for w in ("bn_ready", "mv_ready", "var_ready", "rstd_ready",
                                                "norm_ready")] for k in ("x", "x1")}
        x1_biased = sem("x1_biased")
        sp_passed = sem("sp_passed")
        ga_ready, ga_copied, gate_chain, gap_ready, gap_exp_ready, h_ready, h_t, h_hi, h_lo = map(
            sem, ("ga_ready", "ga_copied", "gate_chain", "gap_ready", "gap_exp_ready", "h_ready",
                  "h_t", "h_hi", "h_lo"))
        block = stack.enter_context(nc.Block())

        @block.sync
        def _(sp):
            def pass_when(ready, n):
                wait(sp, ready, n)
                sp.sem_inc(sp_passed, 1)

            def transpose_halves(dst, src, hi_ready, lo_ready, n, done):
                for part, ready in enumerate((hi_ready, lo_ready)):
                    pass_when(ready, n)
                    sp.dma_start_transpose(dst(part), src[:, part, :]).then_inc(done, 16)

            def probs_out(j, v, src, par, col):
                transpose_halves(lambda part: attnT[par][:, part, :, bass.ds(col * P, P)],
                                 src, probs_hi, probs_lo, j + 1, probs_t[v])

            def load_x(s, u):
                sp.dma_start(x_in[u][:], x_tiles[s]).then_inc(x_loaded[u], 16)

            sp.dma_start(wqk_in[:, 0, :], Wq).then_inc(wqk_loaded, 16)
            sp.dma_start(wqk_in[:, 1, :], Wk).then_inc(wqk_loaded, 16)
            for pair in range(4):
                sp.dma_start(first_ctx[pair], ctx_pairs[pair]).then_inc(first_ctx_loaded[pair], 16)
            for n, v in enumerate((bq, bk)):
                sp.dma_start(bqk[:, n:n + 1], v.rearrange("(p a) -> p a", a=1)) \
                    .then_inc(small_loaded, 16)
            for n, v in enumerate((g_xattn, g_ffn)):
                sp.dma_start(g_in[:, n:n + 1], v.partition_broadcast(P)).then_inc(small_loaded, 16)
            load_x(0, 0)
            for t in range(0, TILES, 2):
                sp.dma_start(w_in[:, t:t + 2, :], W.rearrange("(t p) m -> p t m", p=P)[:, t:t + 2, :]) \
                    .then_inc(w_loaded[t // 2], 16)
            sp.dma_start(lora_a_in[:], lora_A.rearrange("e r m -> (e r) m")).then_inc(ab_loaded, 16)
            sp.dma_start(gate_in[0:EX, :], gate_w).then_inc(ab_loaded, 16)
            load_x(1, 1)
            sp.dma_start(gate_bias[:], gate_b.partition_broadcast(P)).then_inc(bias_loaded, 16)
            sp.dma_start(bias_row[:], bias.partition_broadcast(P)).then_inc(bias_loaded, 16)
            sp.wait_ge(wqk_t, 2)
            for t in range(TILES):
                sp.dma_start(lora_b_in[:, t], lora_B.rearrange("e (t p) r -> t p e r", p=P)[t]) \
                    .then_inc(lora_b_loaded, 16)
            sp.wait_ge(ctx_t, 2)
            sp.dma_start(ctx_in[:], ctx_pairs[4]).then_inc(ctx_loaded, 16)
            transpose_halves(lambda part: xT[:, part], row_split, x_hi, x_lo, 1, x_t)
            with sp.Fori(0, TILES // 2) as i:
                for v in range(2):
                    probs_out(2 * i + v, v, probs_splits[v], 0, 2 * i + v)

            def step(s, b, kind, i, u):
                j = TILES * (b + 1) + 4 * i + 2 * u
                col = 4 * i + 2 * u
                if at_least(s, 2):
                    sp.wait_ge(out_half, 2 * s - 2)
                    sp.dma_start(out_tiles[s - 2], out_row[:]).then_inc(out_stored, 16)
                if kind == "softmax":
                    probs_out(j, 0, probs_split, (b + 1) % 2, col)
                pair = 4 * (b + 1) + 2 * i + u
                if kind == "project" and not (isinstance(pair, int) and pair + 1 >= PAIRS):
                    sp.wait_ge(ctx_t, 2 * pair + 2)
                    sp.dma_start(ctx_in[:], ctx_pairs[pair + 1]).then_inc(ctx_loaded, 16)
                if has_next(s):
                    pass_when(attn_ready, 2 * s + 2)
                    transpose_halves(lambda part: xT[:, part], row_split, x_hi, x_lo, s + 2, x_t)
                if not (isinstance(s, int) and s + 2 >= STEPS):
                    sp.wait_ge(x1_half, 2 * s + 2)
                    load_x(s + 2, u)
                if kind == "softmax":
                    probs_out(j + 1, 1, probs_split, (b + 1) % 2, col + 1)
                pass_when(ffn_ready, 2 * s - 2)
                transpose_halves(lambda part: x1T[u][:, part], row_split, x1_hi, x1_lo, s + 1, x1_t)

            run_steps(sp, step, straight=(4,))
            sp.wait_ge(out_half, 2 * STEPS - 2)
            sp.dma_start(out_tiles[STEPS - 2], out_row[:]).then_inc(out_stored, 16)
            for h in range(2):
                sp.wait_ge(out_half, 2 * STEPS - 1 + h)
                sp.dma_start(out_tiles[STEPS - 1][:, h * BANK:(h + 1) * BANK], half(out_row, h)) \
                    .then_inc(out_stored, 16)
            sp.wait_ge(out_stored, 16 * (STEPS + 1))

        @block.gpsimd
        def _(pool):
            pool.memset(ident[:], 0.0).then_inc(ident_zero, 1)
            pool.wait_ge(ident_zero, 1)
            pool.affine_select(out=ident[:], in_=ident[:], compare_op=ALU.not_equal, fill=1.0,
                               base=0, pattern=[[-1, P]], channel_multiplier=1) \
                .then_inc(ident_ready, 1)
            pool.memset(minus_half[:], -0.5).then_inc(consts_ready, 1)
            pool.memset(bound[:], 0.0).then_inc(consts_ready, 1)
            pool.iota(iota_i[:], pattern=[[1, EX]], base=0, channel_multiplier=0) \
                .then_inc(consts_ready, 1)
            pool.wait_ge(consts_ready, 3)
            pool.tensor_copy(iota[:], iota_i[:]).then_inc(consts_ready, 1)
            def rsqrt(k, n):
                _, _, var, rstd = ln[k]
                pool.wait_ge(ln_sem[k][2], n + 1)
                pool.tensor_tensor(rstd[:], var[:], minus_half[:], ALU.pow) \
                    .then_inc(ln_sem[k][3], 1)

            rsqrt("x", 0)
            pool.wait_ge(tanh_ready, 1)
            pool.wait_ge(bias_loaded, 32)
            pool.tensor_scalar(bias_row[:], bias_row[:], tanh_g[:, 1:2], 1.0, ALU.mult, ALU.mult) \
                .then_inc(bias_row_ready, 1)
            pool.wait_ge(dve_bound, 1)
            pool.partition_all_reduce(bound_all[:], bound[:], P, RMAX).then_inc(bound_reduced, 1)
            pool.wait_ge(bias_row_ready, 1)

            def step(s, b, kind, i, u):
                if has_next(s):
                    rsqrt("x", s + 1)
                rsqrt("x1", s)
                pool.wait_ge(ln_sem["x1"][4], s + 1)
                pool.tensor_tensor(x1[u][:], x1[u][:], bias_row[:], ALU.add).then_inc(x1_biased, 1)

            run_steps(pool, step)

        @block.scalar
        def _(act):
            def hi_out(dst, src, ready, n, done, scale=1.0):
                act.wait_ge(ready, n)
                act.activation(dst, src, ACT.Copy, scale=scale).then_inc(done, 1)

            def ctx_tile(f, ps, at):
                hi_out(ctxT[:, 0, :, at * P:at * P + P], ps.rearrange("p (k n) -> p k n", k=KC),
                       ctx_t, f + 1, ctx_hi)

            def k_out(g, i, ps):
                act.wait_ge(k_ready, g + 1)
                act.activation(kT[:, 0, bass.ds(i * BANK, BANK)], half(ps, 0), ACT.Identity,
                               bias=bqk[:, 1:2]).then_inc(k_hi, 1)

            def q_out(g, i, ps):
                act.wait_ge(q_ready, g + 1)
                act.activation(qT[:, bass.ds(i * BANK, BANK)], half(ps, 1), ACT.Identity,
                               bias=bqk[:, 0:1]).then_inc(q_copied, 1)

            def exp(j, v, ps, row, lo_before):
                act.wait_ge(max_ready, j + 1)
                wait(act, probs_lo, lo_before)
                act.activation(row, ps[:], ACT.Exp, bias=neg_max[:, v:v + 1],
                               accum_out=row_sum[:, v:v + 1]).then_inc(exp_ready, 1)

            def probs_out(j, v, row, split, *t_before):
                act.wait_ge(inv_ready, j + 1)
                if t_before:
                    wait(act, *t_before)
                act.activation(split[:, 0, :], row, ACT.Copy, scale=inv_sum[:, v:v + 1]) \
                    .then_inc(probs_hi, 1)

            def norm_out(k, n, t_before, hi):
                act.wait_ge(ln_sem[k][4], n + 1)
                wait(act, *t_before)
                act.activation(row_split[:, 0, :], row_norm[:], ACT.Copy).then_inc(hi, 1)

            def prep(s, h):
                for (at_h, _), (n, job) in zip(PREP_AT[s], list(enumerate(PREP))[PREP_FIRST[s]:]):
                    if at_h == h:
                        dst, src, by = prep_parts(n, 0)
                        hi_out(dst, src, prep_t, n + 1, prep_hi, scale=by)

            for n in range(2):
                hi_out(wqkT[:, n, 0], half(ps_t, n).rearrange("p (k d) -> p k d", k=KC),
                       wqk_t, n + 1, wqk_hi)
            act.wait_ge(small_loaded, 16 * 4)
            act.activation(tanh_g[:], g_in[:], ACT.Tanh).then_inc(tanh_ready, 1)
            for f in range(TILES // 2):
                ctx_tile(f, first_ps(f), f)
            norm_out("x", 0, (x_t, 0), x_hi)
            k_out(0, 0, ps_score)
            q_out(0, 0, ps_score)
            for f in range(TILES // 2, TILES):
                ctx_tile(f, first_ps(f), f - TILES // 2)
            k_out(1, 1, ps_attn)
            q_out(1, 1, ps_attn)

            def bound_w(t, n):
                act.wait_ge(act_bound, n)
                act.activation(ps_attn[:], w_in[:, t, :], ACT.Abs,
                               accum_out=bound_parts[:, bass.ds(t, 1)]).then_inc(act_bound, 1)

            act.wait_ge(ab_loaded, 16 * 2)
            act.wait_ge(k_lo, 2)
            act.wait_ge(q_copied, 2)
            act.activation(ps_attn[:], lora_a_in[:], ACT.Abs, accum_out=bound_parts[:, 8:9]) \
                .then_inc(act_bound, 1)
            act.wait_ge(act_bound, 1)
            act.activation(ps_attn[0:EX, :], gate_in[0:EX, :], ACT.Abs,
                           accum_out=bound_parts[0:EX, 9:10]).then_inc(act_bound, 1)
            for n in range(TILES // 2):
                act.wait_ge(w_loaded[n], 16)
            exp(0, 0, ps_score, exp_rows[0], 0)
            bound_w(0, 2)
            probs_out(0, 0, exp_rows[0], probs_splits[0])
            exp(1, 1, ps_ffn, exp_rows[1], 0)
            bound_w(1, 3)

            def first_softmax(i):
                for v, ps in ((0, ps_score), (1, ps_ffn)):
                    j = 2 * i + v
                    probs_out(j - 1, 1 - v, exp_rows[1 - v], probs_splits[1 - v],
                              probs_t[1 - v], 32 * (i - 1 + v))
                    exp(j, v, ps, exp_rows[v], j - 1)
                    bound_w(j, j + 2)

            first_softmax(1)
            with act.Fori(2, TILES // 2) as i:
                first_softmax(i)
            probs_out(TILES - 1, 1, exp_rows[1], probs_splits[1],
                      probs_t[1], 32 * (TILES // 2 - 1))

            def step(s, b, kind, i, u):
                j = TILES * (b + 1) + 4 * i + 2 * u
                pair = TILES // 2 * (b + 1) + 2 * i + u
                if isinstance(s, int) and s == 0:
                    act.wait_ge(scales_ready, 10)
                if isinstance(s, int) and s in PREP_AT:
                    prep(s, 0)
                if kind == "softmax":
                    exp(j, 0, ps_score, exp_row[:], j)
                if has_next(s):
                    norm_out("x", s + 1, (x1_t, 32 * s), x_hi)
                if kind == "softmax":
                    probs_out(j, 0, exp_row[:], probs_split, probs_t[1], 32 * pair)
                if at_least(s, 1):
                    act.wait_ge(gap_ready, s)
                    act.activation(gap_exp[:], gap[:], ACT.Exp).then_inc(gap_exp_ready, 1)
                if kind == "softmax":
                    exp(j + 1, 1, ps_t, exp_row[:], j + 1)
                if isinstance(s, int) and s in PREP_AT:
                    prep(s, 1)
                if kind == "project":
                    for v in range(2):
                        ctx_tile(j + v, half(ps_t, v), 2 * u + v)
                if at_least(s, 1):
                    hi_out(hT[:, 0, :], ps_ffn[:, BANK:BANK + ER], h_t, s, h_hi)
                if kind == "softmax":
                    probs_out(j + 1, 1, exp_row[:], probs_split, probs_t[0], 32 * (pair + 1))
                norm_out("x1", s, (x_t, 32 * (s + 2) if has_next(s) else 0), x1_hi)
                if kind == "project" and u == 1:
                    k_out(2 * (b + 1) + i, i, ps_score)
                    q_out(2 * (b + 1) + i, i, ps_score)

            run_steps(act, step)
            act.wait_ge(gap_ready, STEPS)
            act.activation(gap_exp[:], gap[:], ACT.Exp).then_inc(gap_exp_ready, 1)
            hi_out(hT[:, 0, :], ps_ffn[:, BANK:BANK + ER], h_t, STEPS, h_hi)

        @block.vector
        def _(dve):
            def lo_out(dst, hi, src, ready, n, done, scale=1.0):
                dve.wait_ge(ready, n)
                dve.scalar_tensor_tensor(out=dst, in0=src, scalar=scale, in1=hi, op0=ALU.mult,
                                         op1=ALU.subtract).then_inc(done, 1)

            def ctx_tile(f, ps, at):
                cols = slice(at * P, at * P + P)
                lo_out(ctxT[:, 1, :, cols], ctxT[:, 0, :, cols].bitcast(F32),
                       ps.rearrange("p (k n) -> p k n", k=KC), ctx_hi, f + 1, ctx_lo)

            def k_out(g, i, ps):
                cols = bass.ds(i * BANK, BANK)
                dve.wait_ge(k_hi, g + 1)
                dve.scalar_tensor_tensor(out=kT[:, 1, cols], in0=half(ps, 0),
                                         scalar=bqk[:, 1:2], in1=kT[:, 0, cols].bitcast(F32),
                                         op0=ALU.add, op1=ALU.subtract).then_inc(k_lo, 1)

            def q_split(j, v, col):
                wait(dve, scores_ready, j - 1)
                src = qT[:, bass.ds(col * P, P)]
                dve.tensor_copy(q_tile[v][:, 0, :], src).then_inc(q_hi, 1)
                dve.wait_ge(q_hi, j + 1)
                dve.tensor_tensor(q_tile[v][:, 1, :], src, q_tile[v][:, 0, :].bitcast(F32),
                                  ALU.subtract).then_inc(q_lo, 1)

            def row_max(j, v, ps):
                dve.wait_ge(scores_ready, j + 1)
                dve.tensor_reduce(neg_max[:, v:v + 1], ps[:], AX.X, ALU.max, negate=True) \
                    .then_inc(max_ready, 1)

            def inv_row_sum(j, v):
                dve.wait_ge(exp_ready, j + 1)
                dve.tensor_scalar(sum_scaled[:, v:v + 1], row_sum[:, v:v + 1], 1.0 / PROB_SCALE,
                                  None, ALU.mult).then_inc(sum_ready, 1)
                dve.wait_ge(sum_ready, j + 1)
                dve.reciprocal(inv_sum[:, v:v + 1], sum_scaled[:, v:v + 1]).then_inc(inv_ready, 1)

            def probs_out(j, v, row, split):
                lo_out(split[:, 1, :], split[:, 0, :], row, probs_hi, j + 1, probs_lo,
                       scale=inv_sum[:, v:v + 1])

            def ln_bn(k, src, h):
                dve.bn_stats(ln[k][0][:, 6 * h:6 * h + 6], half(src, h)).then_inc(ln_sem[k][0], 1)

            def ln_var(k, n):
                bn, mv, var, _ = ln[k]
                dve.wait_ge(ln_sem[k][0], 2 * n + 2)
                dve.memset(wait_word[:], 0.0)
                dve.bn_aggr(mv[:], bn[:]).then_inc(ln_sem[k][1], 1)
                dve.wait_ge(ln_sem[k][1], n + 1)
                dve.tensor_scalar(var[:], mv[:, 1:2], EPS, NORM_SCALE ** -2, ALU.add, ALU.mult) \
                    .then_inc(ln_sem[k][2], 1)

            def ln_norm(k, n, src):
                _, mv, _, rstd = ln[k]
                dve.wait_ge(ln_sem[k][3], n + 1)
                dve.tensor_scalar(row_norm[:], src[:], mv[:, 0:1], rstd[:], ALU.subtract,
                                  ALU.mult).then_inc(ln_sem[k][4], 1)

            def norm_out(n, hi, lo):
                dve.wait_ge(hi, n + 1)
                dve.tensor_tensor(row_split[:, 1, :], row_norm[:], row_split[:, 0, :],
                                  ALU.subtract).then_inc(lo, 1)

            def x_stats(s, u, loads):
                dve.wait_ge(x_loaded[u], 16 * loads)
                for h in range(2):
                    ln_bn("x", x_in[u], h)
                ln_var("x", s)

            def residual(s, u, h):
                dve.wait_ge(attn_ready, 2 * s + h + 1)
                wait(dve, out_half, 2 * s - 2)
                dve.scalar_tensor_tensor(out=half(x1[u], h), in0=half(ps_attn, h),
                                         scalar=attn_coef[:], in1=half(x_in[u], h),
                                         op0=ALU.mult, op1=ALU.add).then_inc(x1_half, 1)
                dve.wait_ge(x1_half, 2 * s + h + 1)
                ln_bn("x1", x1[u], h)

            def finish(s, u):
                dve.wait_ge(x1_biased, s + 1)
                wait(dve, out_stored, 16 * s)
                for h in range(2):
                    dve.wait_ge(ffn_ready, 2 * s + h + 1)
                    dve.scalar_tensor_tensor(out=half(out_row, h), in0=half(ps_ffn, h),
                                             scalar=ffn_coef[:], in1=half(x1[u], h),
                                             op0=ALU.mult, op1=ALU.add).then_inc(out_half, 1)

            def gates(s):
                def link(ins):
                    ins.then_inc(gate_chain, 1)

                def linked(n):
                    dve.wait_ge(gate_chain, GATE_LINKS * s + n)

                dve.wait_ge(ga_ready, s + 1)
                dve.tensor_copy(ga[:], ps_ffn[:, BANK:BANK + ER + EX]).then_inc(ga_copied, 1)
                dve.wait_ge(ga_copied, s + 1)
                link(dve.scalar_tensor_tensor(out=logits[:], in0=ga[:, ER:ER + EX],
                                              scalar=logit_coef[:], in1=gate_bias[:],
                                              op0=ALU.mult, op1=ALU.add))
                linked(1)
                dve.memset(wait_word[:], 0.0)
                link(dve.max(top[:], logits[:]))
                linked(2)
                dve.tensor_tensor(gap[:], top[:, 1:2], top[:, 0:1], ALU.subtract) \
                    .then_inc(gap_ready, 1)
                link(dve.max_index(top_idx[:], top[:], logits[:]))
                linked(3)
                link(dve.tensor_copy(top_idx_f[:], top_idx[:, 0:2]))
                dve.wait_ge(gap_exp_ready, s + 1)
                link(dve.tensor_scalar(gate_den[:], gap_exp[:], 1.0, None, ALU.add))
                linked(5)
                link(dve.reciprocal(gate_inv[:], gate_den[:]))
                linked(6)
                link(dve.tensor_scalar(gate_top[:, 0:1], gate_inv[:], lora_coef[:], None, ALU.mult))
                linked(7)
                link(dve.tensor_tensor(gate_top[:, 1:2], gate_top[:, 0:1], gap_exp[:], ALU.mult))
                link(dve.tensor_scalar(gate_of[:, 0, :], iota[:], top_idx_f[:, 0:1],
                                       gate_top[:, 0:1], ALU.is_equal, ALU.mult))
                linked(8)
                link(dve.tensor_scalar(gate_of[:, 1, :], iota[:], top_idx_f[:, 1:2],
                                       gate_top[:, 1:2], ALU.is_equal, ALU.mult))
                linked(10)
                link(dve.tensor_tensor(gate_of[:, 2, :], gate_of[:, 0, :], gate_of[:, 1, :],
                                       ALU.add))
                linked(11)
                wait(dve, h_t, s)
                dve.tensor_tensor(h_row[:].rearrange("p (e r) -> p e r", e=EX),
                                  ga[:, 0:ER].rearrange("p (e r) -> p e r", e=EX),
                                  gate_of[:, 2, :].unsqueeze(2).to_broadcast([P, EX, R]),
                                  ALU.mult).then_inc(h_ready, 1)

            def h_out(s):
                lo_out(hT[:, 1, :], hT[:, 0, :].bitcast(F32), ps_ffn[:, BANK:BANK + ER],
                       h_hi, s + 1, h_lo)

            def prep(s, h):
                for (at_h, _), (n, job) in zip(PREP_AT[s], list(enumerate(PREP))[PREP_FIRST[s]:]):
                    if at_h == h:
                        dst, src, by = prep_parts(n, 1)
                        hi = prep_parts(n, 0)[0]
                        lo_out(dst, hi.bitcast(F32) if PREP[n][0] == "lora_b" else hi, src,
                               prep_hi, n + 1, prep_lo, scale=by)

            def weight_scales_first():
                dve.wait_ge(act_bound, 2 + TILES)
                dve.wait_ge(consts_ready, 4)
                dve.tensor_reduce(bound[:, 0:1], bound_parts[:, 0:8], AX.X, ALU.max) \
                    .then_inc(scales_ready, 1)
                dve.tensor_copy(bound[:, 1:2], bound_parts[:, 8:9]).then_inc(scales_ready, 1)
                dve.wait_ge(scales_ready, 2)
                dve.tensor_tensor(bound[0:EX, 1:2], bound_parts[0:EX, 8:9], bound_parts[0:EX, 9:10],
                                  ALU.max).then_inc(dve_bound, 1)

            def weight_scales():
                dve.wait_ge(bound_reduced, 1)
                dve.tensor_scalar(bound_low[:], bound_all[:], 2.0 ** -60, None, ALU.max) \
                    .then_inc(scales_ready, 1)
                dve.wait_ge(scales_ready, 3)
                dve.tensor_scalar(pow2[:].bitcast(U32), bound_low[:].bitcast(U32), EXPONENT, None,
                                  ALU.bitwise_and).then_inc(scales_ready, 1)
                dve.wait_ge(scales_ready, 4)
                dve.reciprocal(inv_pow2[:], pow2[:]).then_inc(scales_ready, 1)
                dve.wait_ge(scales_ready, 5)
                dve.wait_ge(tanh_ready, 1)
                dve.tensor_scalar(attn_coef[:], tanh_g[:, 0:1], 1.0 / (NORM_SCALE * PROB_SCALE),
                                  None, ALU.mult).then_inc(scales_ready, 1)
                dve.tensor_scalar(ffn_coef[:], pow2[:, 0:1], tanh_g[:, 1:2],
                                  1.0 / (NORM_SCALE * W_TOP), ALU.mult, ALU.mult) \
                    .then_inc(scales_ready, 1)
                dve.tensor_scalar(logit_coef[:], pow2[:, 1:2], 1.0 / (NORM_SCALE * W_TOP), None,
                                  ALU.mult).then_inc(scales_ready, 1)
                dve.tensor_scalar(lora_coef[:], pow2[:, 1:2], inv_pow2[:, 0:1], None, ALU.mult) \
                    .then_inc(scales_ready, 1)
                dve.tensor_scalar(scale[:], inv_pow2[:], W_TOP, None, ALU.mult) \
                    .then_inc(scales_ready, 1)
                dve.wait_ge(scales_ready, 10)

            for n in range(2):
                lo_out(wqkT[:, n, 1], wqkT[:, n, 0].bitcast(F32),
                       half(ps_t, n).rearrange("p (k d) -> p k d", k=KC), wqk_hi, n + 1, wqk_lo)
            for f in range(TILES // 2):
                ctx_tile(f, first_ps(f), f)
            x_stats(0, 0, 1)
            ln_norm("x", 0, x_in[0])
            dve.wait_ge(small_loaded, 16 * 4)
            norm_out(0, x_hi, x_lo)
            k_out(0, 0, ps_score)
            dve.wait_ge(q_copied, 1)
            for j in range(2):
                q_split(j, j, j)
            for f in range(TILES // 2, TILES):
                ctx_tile(f, first_ps(f), f - TILES // 2)
            k_out(1, 1, ps_attn)
            dve.wait_ge(q_copied, 2)
            row_max(0, 0, ps_score)
            q_split(2, 0, 2)
            inv_row_sum(0, 0)
            row_max(1, 1, ps_ffn)
            probs_out(0, 0, exp_rows[0], probs_splits[0])
            with dve.Fori(1, TILES // 2 - 1) as i:
                for v, ps in ((0, ps_score), (1, ps_ffn)):
                    j = 2 * i + v
                    q_split(j + 1, 1 - v, j + 1)
                    inv_row_sum(j - 1, 1 - v)
                    row_max(j, v, ps)
                    probs_out(j - 1, 1 - v, exp_rows[1 - v], probs_splits[1 - v])
            for j, ps in ((TILES - 2, ps_score), (TILES - 1, ps_ffn)):
                if j + 1 < TILES:
                    q_split(j + 1, 1, j + 1)
                inv_row_sum(j - 1, (j - 1) % 2)
                row_max(j, j % 2, ps)
                probs_out(j - 1, (j - 1) % 2, exp_rows[(j - 1) % 2], probs_splits[(j - 1) % 2])
            inv_row_sum(TILES - 1, 1)
            weight_scales_first()
            probs_out(TILES - 1, 1, exp_rows[1], probs_splits[1])
            weight_scales()

            def step(s, b, kind, i, u):
                j = TILES * (b + 1) + 4 * i + 2 * u
                col = 4 * i + 2 * u
                preparing = isinstance(s, int) and s in PREP_AT
                if preparing:
                    prep(s, 0)
                if kind == "softmax":
                    if u == 0:
                        dve.wait_ge(q_copied, 2 * (b + 2))
                    q_split(j, 0, col)
                    q_split(j + 1, 1, col + 1)
                if at_least(s, 2):
                    finish(s - 2, u)
                if has_next(s):
                    dve.wait_ge(x_loaded[1 - u], 8 * (s - u) + 16 * (1 + u))
                    for h in range(2):
                        ln_bn("x", x_in[1 - u], h)
                    ln_var("x", s + 1)
                if kind == "softmax":
                    row_max(j, 0, ps_score)
                if has_next(s):
                    ln_norm("x", s + 1, x_in[1 - u])
                residual(s, u, 0)
                if kind == "softmax":
                    inv_row_sum(j, 0)
                    row_max(j + 1, 1, ps_t)
                if at_least(s, 1):
                    gates(s - 1)
                if has_next(s):
                    norm_out(s + 1, x_hi, x_lo)
                if kind == "softmax":
                    probs_out(j, 0, exp_row[:], probs_split)
                if preparing:
                    prep(s, 1)
                if kind == "project":
                    for v in range(2):
                        ctx_tile(j + v, half(ps_t, v), 2 * u + v)
                residual(s, u, 1)
                ln_var("x1", s)
                if at_least(s, 1):
                    h_out(s - 1)
                if kind == "softmax":
                    inv_row_sum(j + 1, 1)
                    probs_out(j + 1, 1, exp_row[:], probs_split)
                ln_norm("x1", s, x1[u])
                norm_out(s, x1_hi, x1_lo)
                if kind == "project" and u == 1:
                    k_out(2 * (b + 1) + i, i, ps_score)

            run_steps(dve, step)
            finish(STEPS - 2, 0)
            gates(STEPS - 1)
            h_out(STEPS - 1)
            finish(STEPS - 1, 1)

        @block.tensor
        def _(pe):
            PASSES = ((0, 0), (0, 1), (1, 0))

            def product(ps, lhs, rhs, first, last):
                for n, (a, c) in enumerate(PASSES):
                    mm = pe.matmul(ps, lhs(a), rhs(c), start=first and n == 0,
                                   stop=last and n == len(PASSES) - 1)
                return mm

            def transposes(h, blocks):
                for n, src in enumerate(blocks):
                    mm = pe.transpose(ps_t[:, h * BANK + n * P:h * BANK + (n + 1) * P], src, ident[:])
                return mm

            def attend(h, par, k):
                return product(half(ps_attn, h), lambda a: xT[:, a, k, :],
                               lambda c: attnT[par][:, c, k, h * BANK:(h + 1) * BANK],
                               k == 0, k == KD - 1)

            def linear(u, h, ks):
                for k in ks:
                    product(half(ps_ffn, h), lambda a: x1T[u][:, a, k, :],
                            lambda c: wT[:, c, k, h * BANK:(h + 1) * BANK], k == 0, False)

            def gate_products(s, u):
                pe.wait_ge(x1_t, 32 * s + 32)
                wait(pe, out_half, 2 * s)
                for k in range(KD):
                    mm = product(ps_ffn[:, BANK:BANK + ER + EX], lambda a: x1T[u][:, a, k, :],
                                 lambda c: agT[:, c, k, :], k == 0, k == KD - 1)
                mm.then_inc(ga_ready, 1)

            def gated_transpose(s):
                pe.wait_ge(h_ready, s + 1)
                pe.transpose(ps_ffn[:, BANK:BANK + ER], h_row[:], ident[:]).then_inc(h_t, 1)

            def lora(h):
                product(half(ps_ffn, h), lambda a: hT[:, a, :],
                        lambda c: bT[:, c, h * BANK:(h + 1) * BANK], False, True) \
                    .then_inc(ffn_ready, 1)

            def scores(j, v, ps):
                pe.wait_ge(q_lo, j + 1)
                for h in range(2):
                    mm = product(half(ps, h), lambda a: q_tile[v][:, a, :],
                                 lambda c: kT[:, c, h * BANK:(h + 1) * BANK], True, True)
                mm.then_inc(scores_ready, 1)

            def ctx_transpose(src, ps):
                for n in range(KC):
                    mm = pe.transpose(ps[:, n * P:(n + 1) * P], src[:, n * P:(n + 1) * P], ident[:])
                mm.then_inc(ctx_t, 1)

            def project(which, ps):
                for k in range(KC):
                    mm = product(half(ps, 1 - which), lambda a: wqkT[:, which, a, k, :],
                                 lambda c: ctxT[:, c, k, :], k == 0, k == KC - 1)
                mm.then_inc((q_ready, k_ready)[which], 1)

            def prep_job(n, free):
                name, at = PREP[n]
                free()
                if name == "lora_b":
                    mm = transposes(n % 2, [lora_b_in[:, HB * at + t].rearrange("p e r -> p (e r)")
                                            for t in range(HB)])
                elif name == "lora_a":
                    mm = transposes(n % 2, [lora_a_in[:, (HB * at + k) * P:(HB * at + k + 1) * P]
                                            for k in range(HB)])
                elif name == "gate":
                    for k in range(KD):
                        at = n % 2 * BANK + k * EX
                        mm = pe.transpose(ps_t[:, at:at + EX], gate_in[0:EX, k * P:(k + 1) * P],
                                          ident[0:EX, 0:EX])
                else:
                    tile, h = at // 2, at % 2
                    mm = transposes(n % 2, [w_in[:, tile, (HB * h + k) * P:(HB * h + k + 1) * P]
                                            for k in range(HB)])
                mm.then_inc(prep_t, 1)

            pe.wait_ge(ident_ready, 1)
            pe.wait_ge(wqk_loaded, 32)
            for n in range(2):
                transposes(n, [wqk_in[:, n, k * P:(k + 1) * P] for k in range(KC)]) \
                    .then_inc(wqk_t, 1)
            for f in range(TILES):
                if f % 2 == 0:
                    pe.wait_ge(first_ctx_loaded[f // 2], 16)
                if f < 2:
                    pe.wait_ge(wqk_lo, f + 1)
                wait(pe, ctx_lo, f - 3)
                ctx_transpose(first_ctx[f // 2][:, f % 2, :], first_ps(f))
                if f == TILES // 2 - 1:
                    pe.wait_ge(ctx_lo, TILES // 2)
                    project(1, ps_score)
                    project(0, ps_score)
            pe.wait_ge(ctx_lo, TILES)
            project(1, ps_attn)
            project(0, ps_attn)
            pe.wait_ge(k_lo, 2)
            scores(0, 0, ps_score)
            scores(1, 1, ps_ffn)
            with pe.Fori(1, TILES // 2) as i:
                for v, ps in ((0, ps_score), (1, ps_ffn)):
                    pe.wait_ge(exp_ready, 2 * i + v - 1)
                    scores(2 * i + v, v, ps)

            def step(s, b, kind, i, u):
                preparing = isinstance(s, int) and s in PREP_AT
                j = TILES * (b + 1) + 4 * i + 2 * u
                g = 2 * (b + 1) + i
                par = b % 2

                def attend_half(h, between=None):
                    for k in range(KD):
                        mm = attend(h, par, k)
                        if k == KD - 1:
                            mm.then_inc(attn_ready, 1)
                        if k == KD // 2 - 1 and between:
                            between()
                        if preparing and (h, k) in PREP_AT[s]:
                            n = PREP_FIRST[s] + PREP_AT[s].index((h, k))
                            prep_job(n, lambda: prep_free(n))

                def prep_free(n):
                    if n == 0:
                        pe.wait_ge(lora_b_loaded, 16 * TILES)
                    elif n >= 2:
                        pe.wait_ge(prep_lo, n - 1)
                    if s == 1 and n < PREP_FIRST[1] + 2:
                        pe.wait_ge(ctx_lo, TILES + 2)

                def first_scores():
                    if kind == "softmax":
                        if u == 0:
                            pe.wait_ge(k_lo, 2 * (b + 2))
                            pe.wait_ge(q_copied, 2 * (b + 2))
                        pe.wait_ge(exp_ready, j - 1)
                        scores(j, 0, ps_score)

                def ctx_pair():
                    if kind == "project":
                        pe.wait_ge(ctx_loaded, 16 * (4 * (b + 1) + 2 * i + u - 3))
                        if preparing:
                            pe.wait_ge(prep_lo, PREP_FIRST[s] + len(PREP_AT[s]))
                        wait(pe, exp_ready, TILES * (b + 1) if b else 0)
                        pe.wait_ge(ctx_lo, j)
                        for v in range(2):
                            ctx_transpose(ctx_in[:, v, :], half(ps_t, v))

                pe.wait_ge(x_t, 32 * s + 32)
                if u == 0:
                    for done in probs_t:
                        pe.wait_ge(done, 32 * (TILES // 2) * (b + 1))
                wait(pe, x1_half, 2 * s - 1)
                if isinstance(s, int) and s == 0:
                    pe.wait_ge(act_bound, TILES + 2)
                attend_half(0, first_scores)
                if kind == "softmax":
                    if u == 0:
                        pe.wait_ge(ctx_lo, TILES * (b + 2))
                    pe.wait_ge(exp_ready, j)
                    scores(j + 1, 1, ps_t)
                if at_least(s, 1):
                    if isinstance(s, int) and s == 1:
                        pe.wait_ge(prep_lo, 5)
                    gate_products(s - 1, 1 - u)
                wait(pe, x1_half, 2 * s)
                attend_half(1, None if preparing else ctx_pair)
                if preparing:
                    ctx_pair()
                if at_least(s, 1):
                    if isinstance(s, int) and s == 1:
                        pe.wait_ge(prep_lo, len(PREP))
                    wait(pe, out_half, 2 * s - 3)
                    linear(1 - u, 0, range(1))
                    gated_transpose(s - 1)
                    linear(1 - u, 0, range(1, KD))
                if kind == "project" and u == 1:
                    wait(pe, exp_ready, TILES * (b + 1))
                    wait(pe, k_lo, g)
                    wait(pe, q_copied, g)
                    pe.wait_ge(ctx_lo, 4 * g + 4)
                    project(1, ps_score)
                    project(0, ps_score)
                if at_least(s, 1):
                    pe.wait_ge(h_lo, s)
                    lora(0)
                    linear(1 - u, 1, range(KD))
                    lora(1)

            run_steps(pe, step)
            gate_products(STEPS - 1, 1)
            pe.wait_ge(out_half, 2 * STEPS - 3)
            linear(1, 0, range(KD))
            gated_transpose(STEPS - 1)
            pe.wait_ge(h_lo, STEPS)
            lora(0)
            linear(1, 1, range(KD))
            lora(1)


_INS = ["x", "ctx_1024", "g_xattn", "g_ffn", "L0_xattn_Wq", "L0_xattn_bq", "L0_xattn_Wk",
        "L0_xattn_bk", "L0_ffn_W", "L0_ffn_b", "L0_ffn_lora_A", "L0_ffn_lora_B", "L0_ffn_gate_w",
        "L0_ffn_gate_b"]
_OUTS = [((B, L, D), "float32")]


def kernel(**inputs):
    import numpy as _np
    import concourse.bacc as _bacc
    from concourse import mybir as _mybir
    from concourse.bass_utils import run_bass_kernel_spmd as _run

    nc = _bacc.Bacc("TRN2", target_bir_lowering=False, num_devices=1)
    arrays, args = {}, []
    for name in _INS:
        a = _np.ascontiguousarray(inputs[name])
        arrays[f"in_{name}_dram"] = a
        args.append(nc.dram_tensor(f"in_{name}_dram", a.shape, _mybir.dt.from_np(a.dtype),
                                   kind="ExternalInput").ap())
    for i, (shape, dtype) in enumerate(_OUTS):
        dt = _mybir.dt.from_np(_np.dtype(dtype))
        args.append(nc.dram_tensor(f"out_{i}_dram", shape, dt, kind="ExternalOutput").ap())
    flamingo_block(nc, *args)
    r = _run(nc, [arrays], core_ids=[0])
    return r.results[0]["out_0_dram"]
```

```python
from contextlib import ExitStack

import concourse.bass as bass
from concourse import mybir

F32 = mybir.dt.float32
F32R = mybir.dt.float32r
F16 = mybir.dt.float16
U32 = mybir.dt.uint32
I32 = mybir.dt.int32
ALU = mybir.AluOpType
ACT = mybir.ActivationFunctionType
AX = mybir.AxisListType
RMAX = bass.bass_isa.ReduceOp.max

P = 128
BANK = 512
B, L, D = 4, 1024, 1024
N, C, DH = 1024, 512, 128
EX, R = 8, 16
ER = EX * R
EPS = 1e-5

TILES = L // P
STEPS = B * TILES
KD = D // P
KC = C // P
HB = BANK // P

NORM_SCALE = 2.0 ** 10
PROB_SCALE = 2.0 ** 15
W_TOP = 2.0 ** 14
EXPONENT = 0x7F800000
GATE_LINKS = 11

SEGMENTS = [(0, 0, 2, "project", False), (0, 4, 2, "softmax", True),
            (1, 0, 2, "project", True), (1, 4, 2, "softmax", True),
            (2, 0, 2, "project", True), (2, 4, 2, "softmax", True),
            (3, 0, 3, None, True), (3, 6, 1, None, False)]

POOL_W = 2
PREP = [("lora_b", 0), ("lora_b", 1), ("lora_a", 0), ("lora_a", 1), ("gate", 0)]


def run_steps(eng, step, straight=()):
    for n, (b, first, pairs, kind, looped) in enumerate(SEGMENTS):
        base = TILES * b + first
        if looped and n not in straight:
            with eng.Fori(0, pairs) as i:
                for u in range(2):
                    step(base + 2 * i + u, b, kind, i, u)
        else:
            for i in range(pairs):
                for u in range(2):
                    step(base + 2 * i + u, b, kind, i, u)


def wait(eng, sem, value):
    if isinstance(value, int) and value <= 0:
        return
    eng.wait_ge(sem, value)


def at_least(s, n):
    return not isinstance(s, int) or s >= n


def has_next(s):
    return not (isinstance(s, int) and s + 1 >= STEPS)


def flamingo_block(nc, x, ctx_tokens, g_xattn, g_ffn, Wq, bq, Wk, bk, W, bias, lora_A, lora_B,
                   gate_w, gate_b, out):
    x_tiles = x.rearrange("b (t p) d -> (b t) p d", p=P)
    out_tiles = out.rearrange("b (t p) d -> (b t) p d", p=P)
    ctx_pairs = ctx_tokens.rearrange("b (q t p) c -> (b q) p t c", p=P, t=2)
    PAIRS = B * N // (2 * P)

    with ExitStack() as stack:
        def sb(name, shape, dt):
            return stack.enter_context(nc.sbuf_tensor(name, shape, dt))

        def sem(name):
            return stack.enter_context(nc.semaphore(name))

        attnT = [sb(f"attnT{v}", [P, 2, KD, L], F16) for v in range(2)]
        wT = sb("wT", [P, 2, KD, D], F16)
        agT = sb("agT", [P, 2, KD, ER + EX], F16)
        bT = sb("bT", [P, 2, D], F32R)
        xT_tile = sb("xT", [P, 2, KD, P], F16)
        x1T = [sb(f"x1T{u}", [P, 2, KD, P], F16) for u in range(2)]
        ctxT = sb("ctxT", [P, 2, KC, BANK], F32R)
        wqkT = sb("wqkT", [P, 2, 2, KC, DH], F32R)
        kT = sb("kT", [P, 2, N], F32R)
        qT = sb("qT", [P, L], F32)
        q_tile = sb("q_tile", [P, HB, 2, P], F32R)
        hT = q_tile[:, 2]
        ctx_in = sb("ctx_in", [P, 2, C], F32)
        x_in = [sb(f"x_in{u}", [P, D], F32) for u in range(2)]
        x1 = [sb(f"x1_{u}", [P, D], F32) for u in range(2)]
        row_norm = sb("row_norm", [P, D], F32)
        row_split = sb("row_split", [P, 2, D], F16)
        out_row = sb("out_row", [P, D], F32)
        exp_row = sb("exp_row", [P, N], F32)
        probs_split = sb("probs_split", [P, 2, N], F16)
        bias_row = sb("bias_row", [P, D], F32)
        ident = sb("ident", [P, P], F32)
        bqk = sb("bqk", [P, 2], F32)
        g_in = sb("g_in", [P, 2], F32)
        tanh_g = sb("tanh_g", [P, 2], F32)
        bound_parts = sb("bound_parts", [P, 10], F32)
        bound = sb("bound", [P, 2], F32)
        bound_all = sb("bound_all", [P, 2], F32)
        bound_low = sb("bound_low", [P, 2], F32)
        pow2 = sb("pow2", [P, 2], F32)
        inv_pow2 = sb("inv_pow2", [P, 2], F32)
        scale = sb("scale", [P, 2], F32)
        attn_coef = sb("attn_coef", [P, 1], F32)
        ffn_coef = sb("ffn_coef", [P, 1], F32)
        logit_coef = sb("logit_coef", [P, 1], F32)
        lora_coef = sb("lora_coef", [P, 1], F32)
        gate_bias = sb("gate_bias", [P, EX], F32)
        iota_i = sb("iota_i", [P, EX], I32)
        iota = sb("iota", [P, EX], F32)
        minus_half = sb("minus_half", [P, 1], F32)
        neg_max = sb("neg_max", [P, 2], F32)
        row_sum = sb("row_sum", [P, 2], F32)
        sum_scaled = sb("sum_scaled", [P, 2], F32)
        inv_sum = sb("inv_sum", [P, 2], F32)
        ln = {k: (sb(f"{k}_bn", [P, 12], F32), sb(f"{k}_mv", [P, 2], F32),
                  sb(f"{k}_var", [P, 1], F32), sb(f"{k}_rstd", [P, 1], F32)) for k in ("x", "x1")}
        ga = sb("ga", [P, ER + EX], F32)
        logits = sb("logits", [P, EX], F32)
        top = sb("top", [P, 8], F32)
        top_idx = sb("top_idx", [P, 8], U32)
        top_idx_f = sb("top_idx_f", [P, 2], F32)
        wait_word = sb("wait_word", [P, 1], F32)
        gap = sb("gap", [P, 1], F32)
        gap_exp = sb("gap_exp", [P, 1], F32)
        gate_den = sb("gate_den", [P, 1], F32)
        gate_inv = sb("gate_inv", [P, 1], F32)
        gate_top = sb("gate_top", [P, 2], F32)
        gate_of = sb("gate_of", [P, 3, EX], F32)
        h_row = sb("h_row", [P, ER], F32)

        w_in = attnT[1][:].rearrange("p a k m -> p (a k m)").bitcast(F32) \
            .rearrange("p (t m) -> p t m", t=TILES)
        w_split = [r.bitcast(F16).rearrange("p (a m) -> p a m", a=2) for r in
                   [qT[:], bias_row[:]]
                   + [w_in[:, t, :] for t in range(TILES - 2)]]
        w_junk = wT[:].rearrange("p a k m -> p (a k m)").bitcast(F32) \
            .rearrange("p (t m) -> p t m", t=TILES)
        wqk_in = x1[0][:].rearrange("p (a c) -> p a c", a=2)
        lora_b_in = x1[0][:].rearrange("p (t e r) -> p t e r", t=TILES, e=EX)
        lora_a_in = x1[1]
        gate_in = x1T[0][:].rearrange("p a k l -> p (a k l)").bitcast(F32)
        gate_spread = h_row[:, 0:EX * D // P]
        more_ctxT = bT[:].rearrange("p a (k n) -> p a k n", k=KC)
        first_q = [q_tile[:], bT[:, 0, :].rearrange("p (t a n) -> p t a n", t=HB, a=2)]
        first_ctx = [ctx_in[:]] + [t.rearrange("p (t c) -> p t c", t=2) for t in (
            exp_row[:], out_row[:],
            probs_split[:].rearrange("p a n -> p (a n)").bitcast(F32))]
        exp_rows = [exp_row[:], out_row[:], row_norm[:]]
        probs_splits = [probs_split[:], x1T[1][:].rearrange("p a k l -> p a (k l)"), row_split[:]]
        second_xT = out_row[:].bitcast(F16).rearrange("p (a k l) -> p a k l", a=2, k=KD)

        ps_attn = stack.enter_context(nc.psum_tensor("ps_attn", [P, 2 * BANK], F32))
        ps_ffn = stack.enter_context(nc.psum_tensor("ps_ffn", [P, 2 * BANK], F32))
        ps_score = stack.enter_context(nc.psum_tensor("ps_score", [P, 2 * BANK], F32))
        ps_t = stack.enter_context(nc.psum_tensor("ps_t", [P, 2 * BANK], F32))

        def half(ps, h):
            return ps[:, h * BANK:(h + 1) * BANK]

        def xT(s):
            return second_xT if isinstance(s, int) and s == 1 else xT_tile

        def first_ctx_at(f):
            return (more_ctxT, f - HB) if f in (HB, HB + 1) else (ctxT[:], f % 6)

        def first_ps(f):
            return half((ps_t, ps_t, ps_ffn, ps_ffn)[f % 4], f % 2)

        def prep_parts(n, part):
            name, at = PREP[n]
            ps = half(ps_t, n % 2)
            if name == "lora_b":
                return bT[:, part, at * BANK:(at + 1) * BANK], ps, 1.0
            if name == "lora_a":
                return (agT[:, part, HB * at:HB * at + HB, 0:ER],
                        ps.rearrange("p (k n) -> p k n", k=HB), scale[:, 1:2])
            return (agT[:, part, :, ER:ER + EX],
                    ps[:, 0:KD * EX].rearrange("p (k n) -> p k n", k=KD), scale[:, 1:2])

        wqk_loaded, ab_loaded, small_loaded, bias_loaded = map(sem, (
            "wqk_loaded", "ab_loaded", "small_loaded", "bias_loaded"))
        w_loaded = [sem(f"w_loaded{n}") for n in range(TILES // 2)]
        first_ctx_loaded = [sem(f"first_ctx_loaded{n}") for n in range(4)]
        ctx_loaded, lora_b_loaded = sem("ctx_loaded"), sem("lora_b_loaded")
        x_loaded = [sem(f"x_loaded{u}") for u in range(2)]
        out_stored = sem("out_stored")
        consts_ready, ident_zero, ident_ready, bias_row_ready = map(sem, (
            "consts_ready", "ident_zero", "ident_ready", "bias_row_ready"))
        tanh_ready, act_bound, dve_part, bound_reduced = map(sem, (
            "tanh_ready", "act_bound", "dve_part", "bound_reduced"))
        dve_bound, scale_ready = ([sem(f"{n}{c}") for c in range(2)]
                                  for n in ("dve_bound", "scale_ready"))
        wqk_t, wqk_hi, wqk_lo = map(sem, ("wqk_t", "wqk_hi", "wqk_lo"))
        w_hi, w_lo = sem("w_hi"), sem("w_lo")
        pool_w_scaled, pool_w_hi, pool_w_lo = map(sem, ("pool_w_scaled", "pool_w_hi", "pool_w_lo"))
        w_t = [sem(f"w_t{n}") for n in range(3)]
        prep_t, prep_hi, prep_lo = map(sem, ("prep_t", "prep_hi", "prep_lo"))
        ctx_t, ctx_hi, ctx_lo = map(sem, ("ctx_t", "ctx_hi", "ctx_lo"))
        k_ready, q_ready, k_hi, k_lo, q_copied = map(sem, (
            "k_ready", "q_ready", "k_hi", "k_lo", "q_copied"))
        first_q_lo = sem("first_q_lo")
        q_hi, q_lo, scores_ready, max_ready, exp_ready, sum_ready, inv_ready = map(sem, (
            "q_hi", "q_lo", "scores_ready", "max_ready", "exp_ready", "sum_ready", "inv_ready"))
        probs_hi, probs_lo = sem("probs_hi"), sem("probs_lo")
        probs_t = [sem(f"probs_t{v}") for v in range(2)]
        first_probs_t = [sem(f"first_probs_t{v}") for v in range(3)]
        x_hi, x_lo, x_t = map(sem, ("x_hi", "x_lo", "x_t"))
        x1_hi, x1_lo, x1_t = map(sem, ("x1_hi", "x1_lo", "x1_t"))
        attn_ready, x1_half, ffn_ready, out_half = map(sem, (
            "attn_ready", "x1_half", "ffn_ready", "out_half"))
        ln_sem = {k: [sem(f"{k}_{w}") for w in ("bn_ready", "mv_ready", "var_ready", "rstd_ready",
                                                "norm_ready")] for k in ("x", "x1")}
        x1_biased = sem("x1_biased")
        sp_passed = sem("sp_passed")
        ga_ready, ga_copied, gate_chain, gap_ready, gap_exp_ready, h_ready, h_t, h_hi, h_lo = map(
            sem, ("ga_ready", "ga_copied", "gate_chain", "gap_ready", "gap_exp_ready", "h_ready",
                  "h_t", "h_hi", "h_lo"))
        block = stack.enter_context(nc.Block())

        @block.sync
        def _(sp):
            def pass_when(ready, n):
                wait(sp, ready, n)
                sp.sem_inc(sp_passed, 1)

            def transpose_halves(dst, src, hi_ready, lo_ready, n, done):
                for part, ready in enumerate((hi_ready, lo_ready)):
                    pass_when(ready, n)
                    sp.dma_start_transpose(dst(part), src[:, part, :]).then_inc(done, 16)

            def probs_out(j, src, par, col, done):
                transpose_halves(lambda part: attnT[par][:, part, :, bass.ds(col * P, P)],
                                 src, probs_hi, probs_lo, j + 1, done)

            def weights(t):
                hi, lo, n = (pool_w_hi, pool_w_lo, t) if t < POOL_W else (w_hi, w_lo, t - POOL_W)
                transpose_halves(lambda part: wT[:, part, :, t * P:(t + 1) * P], w_split[t],
                                 hi, lo, n + 1, w_t[(t >= POOL_W) + (t >= HB)])

            def x_rows(s):
                transpose_halves(lambda part: xT(s)[:, part], row_split, x_hi, x_lo, s + 1, x_t)

            def load_x(s, u):
                sp.dma_start(x_in[u][:], x_tiles[s]).then_inc(x_loaded[u], 16)

            sp.dma_start(wqk_in[:, 0, :], Wq).then_inc(wqk_loaded, 16)
            sp.dma_start(wqk_in[:, 1, :], Wk).then_inc(wqk_loaded, 16)
            for pair in range(4):
                sp.dma_start(first_ctx[pair], ctx_pairs[pair]).then_inc(first_ctx_loaded[pair], 16)
            for n, v in enumerate((bq, bk)):
                sp.dma_start(bqk[:, n:n + 1], v.rearrange("(p a) -> p a", a=1)) \
                    .then_inc(small_loaded, 16)
            for n, v in enumerate((g_xattn, g_ffn)):
                sp.dma_start(g_in[:, n:n + 1], v.partition_broadcast(P)).then_inc(small_loaded, 16)
            load_x(0, 0)
            for t in range(0, TILES, 2):
                sp.dma_start(w_in[:, t:t + 2, :], W.rearrange("(t p) m -> p t m", p=P)[:, t:t + 2, :]) \
                    .then_inc(w_loaded[t // 2], 16)
            sp.dma_start(lora_a_in[:], lora_A.rearrange("e r m -> (e r) m")).then_inc(ab_loaded, 16)
            sp.dma_start(gate_in[0:EX, :], gate_w).then_inc(ab_loaded, 16)
            sp.dma_start(gate_spread, gate_w.rearrange("e (a n) -> (e a) n", a=P // EX)) \
                .then_inc(ab_loaded, 16)
            x_rows(0)
            load_x(1, 1)
            sp.dma_start(gate_bias[:], gate_b.partition_broadcast(P)).then_inc(bias_loaded, 16)
            sp.wait_ge(wqk_t, 2)
            for t in range(TILES):
                sp.dma_start(lora_b_in[:, t], lora_B.rearrange("e (t p) r -> t p e r", p=P)[t]) \
                    .then_inc(lora_b_loaded, 16)
            for j in range(TILES):
                probs_out(j, probs_splits[j % 3], 0, j, first_probs_t[j % 3] if j < 6
                          else probs_t[j - 6])

            def step(s, b, kind, i, u):
                j = TILES * (b + 1) + 4 * i + 2 * u
                col = 4 * i + 2 * u
                first = isinstance(s, int) and s == 0
                if first:
                    sp.wait_ge(ctx_t, 2)
                    sp.dma_start(ctx_in[:], ctx_pairs[4]).then_inc(ctx_loaded, 16)
                    x_rows(1)
                    for t in range(3):
                        weights(t)
                if isinstance(s, int) and s == 1:
                    for t in range(3, TILES):
                        weights(t)
                if at_least(s, 2):
                    sp.wait_ge(out_half, 2 * s - 2)
                    sp.dma_start(out_tiles[s - 2], out_row[:]).then_inc(out_stored, 16)
                if kind == "softmax":
                    probs_out(j, probs_split, (b + 1) % 2, col, probs_t[0])
                pair = 4 * (b + 1) + 2 * i + u
                if kind == "project" and not (isinstance(pair, int) and pair + 1 >= PAIRS):
                    sp.wait_ge(ctx_t, 2 * pair + 2)
                    sp.dma_start(ctx_in[:], ctx_pairs[pair + 1]).then_inc(ctx_loaded, 16)
                if has_next(s) and not first:
                    pass_when(attn_ready, 2 * s + 2)
                    x_rows(s + 1)
                if not (isinstance(s, int) and s + 2 >= STEPS):
                    sp.wait_ge(x1_half, 2 * s + 2)
                    load_x(s + 2, u)
                if first:
                    sp.wait_ge(w_t[0], 32 * POOL_W)
                    sp.dma_start(bias_row[:], bias.partition_broadcast(P)) \
                        .then_inc(bias_loaded, 16)
                if kind == "softmax":
                    probs_out(j + 1, probs_split, (b + 1) % 2, col + 1, probs_t[1])
                pass_when(ffn_ready, 2 * s - 2)
                transpose_halves(lambda part: x1T[u][:, part], row_split, x1_hi, x1_lo, s + 1, x1_t)

            run_steps(sp, step, straight=(4,))
            sp.wait_ge(out_half, 2 * STEPS - 2)
            sp.dma_start(out_tiles[STEPS - 2], out_row[:]).then_inc(out_stored, 16)
            for h in range(2):
                sp.wait_ge(out_half, 2 * STEPS - 1 + h)
                sp.dma_start(out_tiles[STEPS - 1][:, h * BANK:(h + 1) * BANK], half(out_row, h)) \
                    .then_inc(out_stored, 16)
            sp.wait_ge(out_stored, 16 * (STEPS + 1))

        @block.gpsimd
        def _(pool):
            pool.memset(ident[:], 0.0).then_inc(ident_zero, 1)
            pool.wait_ge(ident_zero, 1)
            pool.affine_select(out=ident[:], in_=ident[:], compare_op=ALU.not_equal, fill=1.0,
                               base=0, pattern=[[-1, P]], channel_multiplier=1) \
                .then_inc(ident_ready, 1)
            pool.memset(minus_half[:], -0.5).then_inc(consts_ready, 1)
            pool.iota(iota_i[:], pattern=[[1, EX]], base=0, channel_multiplier=0) \
                .then_inc(consts_ready, 1)
            pool.wait_ge(consts_ready, 2)
            pool.tensor_copy(iota[:], iota_i[:]).then_inc(consts_ready, 1)
            def rsqrt(k, n):
                _, _, var, rstd = ln[k]
                pool.wait_ge(ln_sem[k][2], n + 1)
                pool.tensor_tensor(rstd[:], var[:], minus_half[:], ALU.pow) \
                    .then_inc(ln_sem[k][3], 1)

            def w_rows(t):
                pool.tensor_scalar(w_in[:, t, :], w_in[:, t, :], scale[:, 0:1], 1.0, ALU.mult,
                                   ALU.mult).then_inc(pool_w_scaled, 1)
                pool.wait_ge(pool_w_scaled, t + 1)
                pool.tensor_copy(w_split[t][:, 0, :], w_in[:, t, :]).then_inc(pool_w_hi, 1)
                pool.wait_ge(pool_w_hi, t + 1)
                pool.tensor_tensor(w_split[t][:, 1, :], w_in[:, t, :], w_split[t][:, 0, :],
                                   ALU.subtract).then_inc(pool_w_lo, 1)

            def reduce_bound(c):
                pool.wait_ge(dve_bound[c], 1)
                pool.partition_all_reduce(bound_all[:, c:c + 1], bound[:, c:c + 1], P, RMAX) \
                    .then_inc(bound_reduced, 1)

            def add_bias(s, u):
                pool.wait_ge(ln_sem["x1"][4], s + 1)
                pool.tensor_tensor(x1[u][:], x1[u][:], bias_row[:], ALU.add).then_inc(x1_biased, 1)

            rsqrt("x", 0)
            reduce_bound(0)
            pool.wait_ge(scale_ready[0], 4)
            w_rows(0)
            reduce_bound(1)

            def step(s, b, kind, i, u):
                if has_next(s):
                    rsqrt("x", s + 1)
                if isinstance(s, int) and s == 0:
                    w_rows(1)
                rsqrt("x1", s)
                if isinstance(s, int) and s == 0:
                    return
                if isinstance(s, int) and s == 1:
                    pool.wait_ge(tanh_ready, 1)
                    pool.wait_ge(bias_loaded, 32)
                    pool.tensor_scalar(bias_row[:], bias_row[:], tanh_g[:, 1:2], 1.0, ALU.mult,
                                       ALU.mult).then_inc(bias_row_ready, 1)
                    pool.wait_ge(bias_row_ready, 1)
                    add_bias(0, 0)
                add_bias(s, u)

            run_steps(pool, step)

        @block.scalar
        def _(act):
            def hi_out(dst, src, ready, n, done, scale=1.0):
                act.wait_ge(ready, n)
                act.activation(dst, src, ACT.Copy, scale=scale).then_inc(done, 1)

            def ctx_tile(f, ps, at, ctxT=ctxT):
                hi_out(ctxT[:, 0, :, at * P:at * P + P], ps.rearrange("p (k n) -> p k n", k=KC),
                       ctx_t, f + 1, ctx_hi)

            def k_out(g, i, ps):
                act.wait_ge(k_ready, g + 1)
                act.activation(kT[:, 0, bass.ds(i * BANK, BANK)], ps, ACT.Identity,
                               bias=bqk[:, 1:2]).then_inc(k_hi, 1)

            def q_out(g, i, ps):
                act.wait_ge(q_ready, g + 1)
                act.activation(qT[:, bass.ds(i * BANK, BANK)], ps, ACT.Identity,
                               bias=bqk[:, 0:1]).then_inc(q_copied, 1)

            def first_q_out(i, ps):
                act.wait_ge(q_ready, i + 1)
                act.activation(first_q[i][:, :, 0, :], ps.rearrange("p (t n) -> p t n", t=HB),
                               ACT.Identity, bias=bqk[:, 0:1]).then_inc(q_copied, 1)

            def exp(j, v, ps, row, lo_before):
                act.wait_ge(max_ready, j + 1)
                wait(act, probs_lo, lo_before)
                act.activation(row, ps[:], ACT.Exp, bias=neg_max[:, v:v + 1],
                               accum_out=row_sum[:, v:v + 1]).then_inc(exp_ready, 1)

            def probs_out(j, v, row, split, *t_before):
                act.wait_ge(inv_ready, j + 1)
                wait(act, *t_before)
                act.activation(split[:, 0, :], row, ACT.Copy, scale=inv_sum[:, v:v + 1]) \
                    .then_inc(probs_hi, 1)

            def norm_out(k, n, t_before, hi):
                act.wait_ge(ln_sem[k][4], n + 1)
                wait(act, *t_before)
                act.activation(row_split[:, 0, :], row_norm[:], ACT.Copy).then_inc(hi, 1)

            def gate_exp(s):
                act.wait_ge(gap_ready, s + 1)
                act.activation(gap_exp[:], gap[:], ACT.Exp).then_inc(gap_exp_ready, 1)

            def h_out(s):
                hi_out(hT[:, 0, :], ps_ffn[:, BANK:BANK + ER], h_t, s + 1, h_hi)

            def prep(jobs):
                for n in jobs:
                    if n == 2:
                        act.wait_ge(scale_ready[1], 8)
                    dst, src, by = prep_parts(n, 0)
                    hi_out(dst, src, prep_t, n + 1, prep_hi, scale=by)

            def bound_rows(at, rows):
                if at >= TILES:
                    act.wait_ge(act_bound, at - 2)
                act.activation(w_junk[:, at % TILES, 0:rows.shape[-1]], rows, ACT.Abs,
                               accum_out=bound_parts[:, at:at + 1]).then_inc(act_bound, 1)

            def bound_w(t):
                act.wait_ge(w_loaded[t // 2], 16)
                bound_rows(t, w_in[:, t, :])

            def w_rows(t):
                if t < 2 + POOL_W:
                    act.wait_ge(pool_w_lo, t - 1)
                else:
                    act.wait_ge(w_lo, t - 1 - POOL_W)
                act.activation(w_split[t][:, 0, :], w_in[:, t, :], ACT.Copy,
                               scale=scale[:, 0:1]).then_inc(w_hi, 1)

            for n in range(2):
                hi_out(wqkT[:, n, 0], half(ps_t, n).rearrange("p (k d) -> p k d", k=KC),
                       wqk_t, n + 1, wqk_hi)
            def first_ctx_tile(f):
                ctx, at = first_ctx_at(f)
                ctx_tile(f, first_ps(f), at, ctx)

            for f in range(6):
                first_ctx_tile(f)
            act.wait_ge(small_loaded, 16 * 4)
            act.activation(tanh_g[:], g_in[:], ACT.Tanh).then_inc(tanh_ready, 1)
            first_q_out(0, half(ps_attn, 1))
            bound_w(1)
            act.wait_ge(k_ready, 1)
            for f in range(6, TILES):
                first_ctx_tile(f)
            norm_out("x", 0, (x_t, 0), x_hi)
            k_out(0, 0, half(ps_attn, 0))
            k_out(1, 1, half(ps_t, 0))
            for t in range(3, 6):
                bound_w(t)
            def first_probs(j):
                probs_out(j, j % 2, exp_rows[j % 3], probs_splits[j % 3],
                          *((x_t, 32) if j == 2 else (first_probs_t[j % 3], 32 * (j // 3))))

            for j in range(TILES):
                exp(j, j % 2, (ps_score, ps_ffn)[j % 2], exp_rows[j % 3], j - 2)
                if j == 2:
                    first_q_out(1, half(ps_t, 1))
                if j in (2, 3):
                    bound_w(4 + j)
                elif j == 4:
                    act.wait_ge(ab_loaded, 16 * 3)
                    bound_rows(8, lora_a_in[:])
                elif j == 5:
                    bound_rows(9, gate_spread)
                if j:
                    first_probs(j - 1)
            first_probs(TILES - 1)

            def step(s, b, kind, i, u):
                j = TILES * (b + 1) + 4 * i + 2 * u
                pair = 1 + TILES // 2 * b + 2 * i + u
                first, second = (isinstance(s, int) and s == n for n in range(2))
                if kind == "softmax":
                    exp(j, 0, ps_score, exp_row[:], j)
                if second:
                    for v in range(2):
                        ctx_tile(j + v, half(ps_t, v), 2 * u + v)
                    gate_exp(0)
                if first:
                    prep(range(2))
                if has_next(s):
                    norm_out("x", s + 1, (first_probs_t[2], 64) if first else (x1_t, 32 * s), x_hi)
                if kind == "softmax":
                    probs_out(j, 0, exp_row[:], probs_split, probs_t[1], 32 * pair)
                if at_least(s, 2):
                    gate_exp(s - 1)
                if kind == "softmax":
                    exp(j + 1, 1, ps_t, exp_row[:], j + 1)
                if first:
                    prep(range(2, 4))
                    w_rows(2)
                    prep(range(4, 5))
                if second:
                    h_out(0)
                if kind == "project" and not second:
                    for v in range(2):
                        ctx_tile(j + v, half(ps_t, v), 2 * u + v)
                if first:
                    w_rows(3)
                if at_least(s, 2):
                    h_out(s - 1)
                if kind == "softmax":
                    probs_out(j + 1, 1, exp_row[:], probs_split, probs_t[0], 32 * (pair + 1))
                norm_out("x1", s, (x_t, 32 * (s + 2) if has_next(s) else 0), x1_hi)
                if first:
                    for t in range(HB, TILES):
                        w_rows(t)
                if kind == "project" and u == 1:
                    k_out(2 * (b + 1) + i, i, half(ps_score, 0))
                    q_out(2 * (b + 1) + i, i, half(ps_score, 1))

            run_steps(act, step)
            gate_exp(STEPS - 1)
            h_out(STEPS - 1)

        @block.vector
        def _(dve):
            def lo_out(dst, hi, src, ready, n, done, scale=1.0):
                dve.wait_ge(ready, n)
                dve.scalar_tensor_tensor(out=dst, in0=src, scalar=scale, in1=hi, op0=ALU.mult,
                                         op1=ALU.subtract).then_inc(done, 1)

            def ctx_tile(f, ps, at, ctxT=ctxT):
                cols = slice(at * P, at * P + P)
                lo_out(ctxT[:, 1, :, cols], ctxT[:, 0, :, cols].bitcast(F32),
                       ps.rearrange("p (k n) -> p k n", k=KC), ctx_hi, f + 1, ctx_lo)

            def k_out(g, i, ps):
                cols = bass.ds(i * BANK, BANK)
                dve.wait_ge(k_hi, g + 1)
                dve.scalar_tensor_tensor(out=kT[:, 1, cols], in0=ps,
                                         scalar=bqk[:, 1:2], in1=kT[:, 0, cols].bitcast(F32),
                                         op0=ALU.add, op1=ALU.subtract).then_inc(k_lo, 1)

            def first_q_out(i, ps):
                dve.wait_ge(q_copied, i + 1)
                dve.scalar_tensor_tensor(out=first_q[i][:, :, 1, :],
                                         in0=ps.rearrange("p (t n) -> p t n", t=HB),
                                         scalar=bqk[:, 0:1],
                                         in1=first_q[i][:, :, 0, :].bitcast(F32),
                                         op0=ALU.add, op1=ALU.subtract).then_inc(first_q_lo, 1)

            def q_split(j, v, col):
                wait(dve, scores_ready, j - 1)
                src = qT[:, bass.ds(col * P, P)]
                dve.tensor_copy(q_tile[:, v, 0, :], src).then_inc(q_hi, 1)
                dve.wait_ge(q_hi, j + 1 - TILES)
                dve.tensor_tensor(q_tile[:, v, 1, :], src, q_tile[:, v, 0, :].bitcast(F32),
                                  ALU.subtract).then_inc(q_lo, 1)

            def row_max(j, v, ps):
                dve.wait_ge(scores_ready, j + 1)
                dve.tensor_reduce(neg_max[:, v:v + 1], ps[:], AX.X, ALU.max, negate=True) \
                    .then_inc(max_ready, 1)

            def inv_row_sum(j, v):
                dve.wait_ge(exp_ready, j + 1)
                dve.tensor_scalar(sum_scaled[:, v:v + 1], row_sum[:, v:v + 1], 1.0 / PROB_SCALE,
                                  None, ALU.mult).then_inc(sum_ready, 1)
                dve.wait_ge(sum_ready, j + 1)
                dve.reciprocal(inv_sum[:, v:v + 1], sum_scaled[:, v:v + 1]).then_inc(inv_ready, 1)

            def probs_out(j, v, row, split):
                lo_out(split[:, 1, :], split[:, 0, :], row, probs_hi, j + 1, probs_lo,
                       scale=inv_sum[:, v:v + 1])

            def ln_bn(k, src, h):
                dve.bn_stats(ln[k][0][:, 6 * h:6 * h + 6], half(src, h)).then_inc(ln_sem[k][0], 1)

            def ln_var(k, n):
                bn, mv, var, _ = ln[k]
                dve.wait_ge(ln_sem[k][0], 2 * n + 2)
                dve.memset(wait_word[:], 0.0)
                dve.bn_aggr(mv[:], bn[:]).then_inc(ln_sem[k][1], 1)
                dve.wait_ge(ln_sem[k][1], n + 1)
                dve.tensor_scalar(var[:], mv[:, 1:2], EPS, NORM_SCALE ** -2, ALU.add, ALU.mult) \
                    .then_inc(ln_sem[k][2], 1)

            def ln_norm(k, n, src):
                _, mv, _, rstd = ln[k]
                dve.wait_ge(ln_sem[k][3], n + 1)
                dve.tensor_scalar(row_norm[:], src[:], mv[:, 0:1], rstd[:], ALU.subtract,
                                  ALU.mult).then_inc(ln_sem[k][4], 1)

            def norm_out(n, hi, lo):
                dve.wait_ge(hi, n + 1)
                dve.tensor_tensor(row_split[:, 1, :], row_norm[:], row_split[:, 0, :],
                                  ALU.subtract).then_inc(lo, 1)

            def x_stats(s, u, loads):
                dve.wait_ge(x_loaded[u], 16 * loads)
                for h in range(2):
                    ln_bn("x", x_in[u], h)
                ln_var("x", s)

            def residual(s, u, h):
                dve.wait_ge(attn_ready, 2 * s + h + 1)
                wait(dve, out_half, 2 * s - 2)
                dve.scalar_tensor_tensor(out=half(x1[u], h), in0=half(ps_attn, h),
                                         scalar=attn_coef[:], in1=half(x_in[u], h),
                                         op0=ALU.mult, op1=ALU.add).then_inc(x1_half, 1)
                dve.wait_ge(x1_half, 2 * s + h + 1)
                ln_bn("x1", x1[u], h)

            def finish(s, u):
                dve.wait_ge(x1_biased, s + 1)
                wait(dve, out_stored, 16 * s)
                for h in range(2):
                    dve.wait_ge(ffn_ready, 2 * s + h + 1)
                    dve.scalar_tensor_tensor(out=half(out_row, h), in0=half(ps_ffn, h),
                                             scalar=ffn_coef[:], in1=half(x1[u], h),
                                             op0=ALU.mult, op1=ALU.add).then_inc(out_half, 1)

            def gates(s):
                def link(ins):
                    ins.then_inc(gate_chain, 1)

                def linked(n):
                    dve.wait_ge(gate_chain, GATE_LINKS * s + n)

                dve.wait_ge(ga_ready, s + 1)
                dve.tensor_copy(ga[:], ps_ffn[:, BANK:BANK + ER + EX]).then_inc(ga_copied, 1)
                dve.wait_ge(ga_copied, s + 1)
                link(dve.scalar_tensor_tensor(out=logits[:], in0=ga[:, ER:ER + EX],
                                              scalar=logit_coef[:], in1=gate_bias[:],
                                              op0=ALU.mult, op1=ALU.add))
                linked(1)
                dve.memset(wait_word[:], 0.0)
                link(dve.max(top[:], logits[:]))
                linked(2)
                dve.tensor_tensor(gap[:], top[:, 1:2], top[:, 0:1], ALU.subtract) \
                    .then_inc(gap_ready, 1)
                link(dve.max_index(top_idx[:], top[:], logits[:]))
                linked(3)
                link(dve.tensor_copy(top_idx_f[:], top_idx[:, 0:2]))
                dve.wait_ge(gap_exp_ready, s + 1)
                link(dve.tensor_scalar(gate_den[:], gap_exp[:], 1.0, None, ALU.add))
                linked(5)
                link(dve.reciprocal(gate_inv[:], gate_den[:]))
                linked(6)
                link(dve.tensor_scalar(gate_top[:, 0:1], gate_inv[:], lora_coef[:], None, ALU.mult))
                linked(7)
                link(dve.tensor_tensor(gate_top[:, 1:2], gate_top[:, 0:1], gap_exp[:], ALU.mult))
                link(dve.tensor_scalar(gate_of[:, 0, :], iota[:], top_idx_f[:, 0:1],
                                       gate_top[:, 0:1], ALU.is_equal, ALU.mult))
                linked(8)
                link(dve.tensor_scalar(gate_of[:, 1, :], iota[:], top_idx_f[:, 1:2],
                                       gate_top[:, 1:2], ALU.is_equal, ALU.mult))
                linked(10)
                link(dve.tensor_tensor(gate_of[:, 2, :], gate_of[:, 0, :], gate_of[:, 1, :],
                                       ALU.add))
                linked(11)
                wait(dve, h_t, s)
                dve.tensor_tensor(h_row[:].rearrange("p (e r) -> p e r", e=EX),
                                  ga[:, 0:ER].rearrange("p (e r) -> p e r", e=EX),
                                  gate_of[:, 2, :].unsqueeze(2).to_broadcast([P, EX, R]),
                                  ALU.mult).then_inc(h_ready, 1)

            def h_out(s):
                lo_out(hT[:, 1, :], hT[:, 0, :].bitcast(F32), ps_ffn[:, BANK:BANK + ER],
                       h_hi, s + 1, h_lo)

            def prep(jobs):
                for n in jobs:
                    name = PREP[n][0]
                    dst, src, by = prep_parts(n, 1)
                    hi = prep_parts(n, 0)[0]
                    lo_out(dst, hi.bitcast(F32) if name == "lora_b" else hi, src,
                           prep_hi, n + 1, prep_lo, scale=by)

            def bound_w(t):
                dve.wait_ge(w_loaded[t // 2], 16)
                dve.tensor_reduce(bound_parts[:, t:t + 1], w_in[:, t, :], AX.X, ALU.max,
                                  apply_absolute_value=True).then_inc(dve_part, 1)

            def bound_of(c):
                dve.wait_ge(act_bound, (TILES - 2, TILES)[c])
                if c == 0:
                    dve.wait_ge(dve_part, 2)
                parts = bound_parts[:, TILES * c:TILES + 2 * c]
                dve.tensor_reduce(bound[:, c:c + 1], parts, AX.X, ALU.max).then_inc(dve_bound[c], 1)

            def scale_of(c):
                col, ready = slice(c, c + 1), scale_ready[c]
                dve.wait_ge(bound_reduced, c + 1)
                dve.tensor_scalar(bound_low[:, col], bound_all[:, col], 2.0 ** -60, None, ALU.max) \
                    .then_inc(ready, 1)
                dve.wait_ge(ready, 1)
                dve.tensor_scalar(pow2[:, col].bitcast(U32), bound_low[:, col].bitcast(U32),
                                  EXPONENT, None, ALU.bitwise_and).then_inc(ready, 1)
                dve.wait_ge(ready, 2)
                dve.reciprocal(inv_pow2[:, col], pow2[:, col]).then_inc(ready, 1)
                dve.wait_ge(ready, 3)
                dve.tensor_scalar(scale[:, col], inv_pow2[:, col], W_TOP, None, ALU.mult) \
                    .then_inc(ready, 1)

            def coefficients():
                ready = scale_ready[1]
                dve.wait_ge(tanh_ready, 1)
                dve.tensor_scalar(attn_coef[:], tanh_g[:, 0:1], 1.0 / (NORM_SCALE * PROB_SCALE),
                                  None, ALU.mult).then_inc(ready, 1)
                dve.tensor_scalar(ffn_coef[:], pow2[:, 0:1], tanh_g[:, 1:2],
                                  1.0 / (NORM_SCALE * W_TOP), ALU.mult, ALU.mult) \
                    .then_inc(ready, 1)
                dve.tensor_scalar(logit_coef[:], pow2[:, 1:2], 1.0 / (NORM_SCALE * W_TOP), None,
                                  ALU.mult).then_inc(ready, 1)
                dve.tensor_scalar(lora_coef[:], pow2[:, 1:2], inv_pow2[:, 0:1], None, ALU.mult) \
                    .then_inc(ready, 1)
                dve.wait_ge(ready, 8)

            def w_rows(t):
                lo_out(w_split[t][:, 1, :], w_split[t][:, 0, :], w_in[:, t, :], w_hi,
                       t - POOL_W + 1, w_lo, scale=scale[:, 0:1])

            for n in range(2):
                lo_out(wqkT[:, n, 1], wqkT[:, n, 0].bitcast(F32),
                       half(ps_t, n).rearrange("p (k d) -> p k d", k=KC), wqk_hi, n + 1, wqk_lo)
            def first_ctx_tile(f):
                ctx, at = first_ctx_at(f)
                ctx_tile(f, first_ps(f), at, ctx)

            for f in range(6):
                first_ctx_tile(f)
            x_stats(0, 0, 1)
            dve.wait_ge(small_loaded, 16 * 4)
            first_q_out(0, half(ps_attn, 1))
            ln_norm("x", 0, x_in[0])
            for f in range(6, TILES):
                first_ctx_tile(f)
            norm_out(0, x_hi, x_lo)
            k_out(0, 0, half(ps_attn, 0))
            k_out(1, 1, half(ps_t, 0))
            bound_w(0)
            def first_probs(j):
                probs_out(j, j % 2, exp_rows[j % 3], probs_splits[j % 3])

            for j in range(TILES):
                row_max(j, j % 2, (ps_score, ps_ffn)[j % 2])
                if j:
                    inv_row_sum(j - 1, (j - 1) % 2)
                if j == 1:
                    bound_w(2)
                elif j == 3:
                    first_q_out(1, half(ps_t, 1))
                elif j == 4:
                    bound_of(0)
                elif j == 5:
                    scale_of(0)
                if j >= 2:
                    first_probs(j - 2)
            bound_of(1)
            inv_row_sum(TILES - 1, 1)
            for j in (TILES - 2, TILES - 1):
                first_probs(j)

            def step(s, b, kind, i, u):
                j = TILES * (b + 1) + 4 * i + 2 * u
                col = 4 * i + 2 * u
                first, second = (isinstance(s, int) and s == n for n in range(2))
                if kind == "softmax":
                    if u == 0:
                        dve.wait_ge(q_copied, 2 * (b + 2))
                    q_split(j, 0, col)
                    q_split(j + 1, 1, col + 1)
                if at_least(s, 2):
                    finish(s - 2, u)
                if has_next(s):
                    dve.wait_ge(x_loaded[1 - u], 8 * (s - u) + 16 * (1 + u))
                    for h in range(2):
                        ln_bn("x", x_in[1 - u], h)
                    ln_var("x", s + 1)
                if kind == "softmax":
                    row_max(j, 0, ps_score)
                if first:
                    prep(range(1))
                if second:
                    for v in range(2):
                        ctx_tile(j + v, half(ps_t, v), 2 * u + v)
                if has_next(s):
                    ln_norm("x", s + 1, x_in[1 - u])
                if second:
                    gates(0)
                if first:
                    prep(range(1, 2))
                    norm_out(s + 1, x_hi, x_lo)
                    scale_of(1)
                    coefficients()
                    prep(range(2, 4))
                    prep(range(4, 5))
                    w_rows(2)
                residual(s, u, 0)
                if second:
                    h_out(0)
                if kind == "softmax":
                    inv_row_sum(j, 0)
                    row_max(j + 1, 1, ps_t)
                if at_least(s, 2):
                    gates(s - 1)
                if has_next(s) and not first:
                    norm_out(s + 1, x_hi, x_lo)
                if kind == "softmax":
                    probs_out(j, 0, exp_row[:], probs_split)
                if kind == "project" and not first and not second:
                    for v in range(2):
                        ctx_tile(j + v, half(ps_t, v), 2 * u + v)
                residual(s, u, 1)
                ln_var("x1", s)
                if first:
                    for v in range(2):
                        ctx_tile(j + v, half(ps_t, v), 2 * u + v)
                if at_least(s, 2):
                    h_out(s - 1)
                if kind == "softmax":
                    inv_row_sum(j + 1, 1)
                    probs_out(j + 1, 1, exp_row[:], probs_split)
                ln_norm("x1", s, x1[u])
                if first:
                    w_rows(3)
                norm_out(s, x1_hi, x1_lo)
                if first:
                    for t in range(HB, TILES):
                        w_rows(t)
                if kind == "project" and u == 1:
                    k_out(2 * (b + 1) + i, i, half(ps_score, 0))

            run_steps(dve, step)
            finish(STEPS - 2, 0)
            gates(STEPS - 1)
            h_out(STEPS - 1)
            finish(STEPS - 1, 1)

        @block.tensor
        def _(pe):
            PASSES = ((0, 0), (0, 1), (1, 0))

            def product(ps, lhs, rhs, first, last):
                for n, (a, c) in enumerate(PASSES):
                    mm = pe.matmul(ps, lhs(a), rhs(c), start=first and n == 0,
                                   stop=last and n == len(PASSES) - 1)
                return mm

            def transposes(h, blocks):
                for n, src in enumerate(blocks):
                    mm = pe.transpose(ps_t[:, h * BANK + n * P:h * BANK + (n + 1) * P], src, ident[:])
                return mm

            def attend(s, par, k, start, width=BANK):
                return product(ps_attn[:, start:start + width], lambda a: xT(s)[:, a, k, :],
                               lambda c: attnT[par][:, c, k, start:start + width],
                               k == 0, k == KD - 1)

            def linear(u, h, ks):
                for k in ks:
                    product(half(ps_ffn, h), lambda a: x1T[u][:, a, k, :],
                            lambda c: wT[:, c, k, h * BANK:(h + 1) * BANK], k == 0, False)

            def gate_products(s, u):
                pe.wait_ge(x1_t, 32 * s + 32)
                wait(pe, out_half, 2 * s)
                for k in range(KD):
                    mm = product(ps_ffn[:, BANK:BANK + ER + EX], lambda a: x1T[u][:, a, k, :],
                                 lambda c: agT[:, c, k, :], k == 0, k == KD - 1)
                mm.then_inc(ga_ready, 1)

            def gated_transpose(s):
                pe.wait_ge(h_ready, s + 1)
                pe.transpose(ps_ffn[:, BANK:BANK + ER], h_row[:], ident[:]).then_inc(h_t, 1)

            def lora(h):
                product(half(ps_ffn, h), lambda a: hT[:, a, :],
                        lambda c: bT[:, c, h * BANK:(h + 1) * BANK], False, True) \
                    .then_inc(ffn_ready, 1)

            def scores(j, v, ps, first=False):
                if first:
                    pe.wait_ge(first_q_lo, j // HB + 1)
                else:
                    pe.wait_ge(q_lo, j + 1 - TILES)
                for h in range(2):
                    if first and j == 0:
                        pe.wait_ge(k_lo, h + 1)
                    mm = product(half(ps, h),
                                 lambda a: (first_q[j // HB][:, j % HB, a, :] if first
                                            else q_tile[:, v, a, :]),
                                 lambda c: kT[:, c, h * BANK:(h + 1) * BANK], True, True)
                mm.then_inc(scores_ready, 1)

            def ctx_transpose(src, ps):
                for n in range(KC):
                    mm = pe.transpose(ps[:, n * P:(n + 1) * P], src[:, n * P:(n + 1) * P], ident[:])
                mm.then_inc(ctx_t, 1)

            def project(which, ps, part=None):
                ctx = (ctxT[:], more_ctxT, ctxT[:, :, :, 0:BANK // 2])[
                    0 if part is None else 1 + part]
                if part is not None:
                    ps = ps[:, part * BANK // 2:(part + 1) * BANK // 2]
                for k in range(KC):
                    mm = product(ps, lambda a: wqkT[:, which, a, k, :],
                                 lambda c: ctx[:, c, k, :], k == 0, k == KC - 1)
                if part != 0:
                    mm.then_inc((q_ready, k_ready)[which], 1)

            def prep_job(n):
                name, at = PREP[n]
                if n >= 2:
                    pe.wait_ge(prep_lo, n - 1)
                if name == "lora_b":
                    pe.wait_ge(lora_b_loaded, 16 * TILES)
                    mm = transposes(n % 2, [lora_b_in[:, HB * at + t].rearrange("p e r -> p (e r)")
                                            for t in range(HB)])
                elif name == "lora_a":
                    mm = transposes(n % 2, [lora_a_in[:, (HB * at + k) * P:(HB * at + k + 1) * P]
                                            for k in range(HB)])
                else:
                    for k in range(KD):
                        at = n % 2 * BANK + k * EX
                        mm = pe.transpose(ps_t[:, at:at + EX], gate_in[0:EX, k * P:(k + 1) * P],
                                          ident[0:EX, 0:EX])
                mm.then_inc(prep_t, 1)

            pe.wait_ge(ident_ready, 1)
            pe.wait_ge(wqk_loaded, 32)
            for n in range(2):
                transposes(n, [wqk_in[:, n, k * P:(k + 1) * P] for k in range(KC)]) \
                    .then_inc(wqk_t, 1)
            for f in range(TILES):
                if f % 2 == 0:
                    pe.wait_ge(first_ctx_loaded[f // 2], 16)
                if f < 2:
                    pe.wait_ge(wqk_lo, f + 1)
                wait(pe, ctx_lo, f - 3)
                ctx_transpose(first_ctx[f // 2][:, f % 2, :], first_ps(f))
            pe.wait_ge(ctx_lo, HB)
            project(0, half(ps_attn, 1))
            project(1, half(ps_attn, 0))
            pe.wait_ge(ctx_lo, 6)
            project(1, half(ps_t, 0), part=0)
            pe.wait_ge(ctx_lo, TILES)
            project(1, half(ps_t, 0), part=1)
            for j in range(TILES):
                wait(pe, exp_ready, j - 1)
                scores(j, j % 2, (ps_score, ps_ffn)[j % 2], first=True)
                if j in (1, 2):
                    project(0, half(ps_t, 1), part=j - 1)
            for n in range(2):
                prep_job(n)

            def step(s, b, kind, i, u):
                first, second = (isinstance(s, int) and s == n for n in range(2))
                j = TILES * (b + 1) + 4 * i + 2 * u
                g = 2 * (b + 1) + i
                par = b % 2

                def attend_half(h, between=None):
                    for k in range(KD):
                        mm = attend(s, par, k, h * BANK)
                        if k == KD - 1:
                            mm.then_inc(attn_ready, 1)
                        if k == KD // 2 - 1 and between:
                            between()

                def first_second_half():
                    for done in first_probs_t:
                        pe.wait_ge(done, 64)
                    for k in range(KD):
                        attend(0, 0, k, BANK, BANK // 2)
                    for n in range(2, 4):
                        prep_job(n)
                    for done in probs_t:
                        pe.wait_ge(done, 32)
                    for k in range(KD):
                        mm = attend(0, 0, k, BANK + BANK // 2, BANK // 2)
                    mm.then_inc(attn_ready, 1)
                    prep_job(4)

                def first_scores():
                    if kind == "softmax":
                        if u == 0:
                            pe.wait_ge(k_lo, 2 * (b + 2))
                            pe.wait_ge(q_copied, 2 * (b + 2))
                        pe.wait_ge(exp_ready, j - 1)
                        scores(j, 0, ps_score)

                def ctx_pair():
                    if kind == "project":
                        pe.wait_ge(ctx_loaded, 16 * (4 * (b + 1) + 2 * i + u - 3))
                        if first:
                            pe.wait_ge(prep_lo, len(PREP))
                        wait(pe, exp_ready, TILES * (b + 1) if b else 0)
                        pe.wait_ge(ctx_lo, j)
                        for v in range(2):
                            ctx_transpose(ctx_in[:, v, :], half(ps_t, v))

                pe.wait_ge(x_t, 32 * s + 32)
                if u == 0:
                    for done in (() if b == 0 else probs_t):
                        pe.wait_ge(done, 32 * (1 + TILES // 2 * b))
                if first:
                    for done, n in zip(first_probs_t, (2, 1, 1)):
                        pe.wait_ge(done, 32 * n)
                wait(pe, x1_half, 2 * s - 1)
                attend_half(0, first_scores)
                if kind == "softmax":
                    if u == 0:
                        pe.wait_ge(ctx_lo, TILES * (b + 2))
                    pe.wait_ge(exp_ready, j)
                    scores(j + 1, 1, ps_t)
                if at_least(s, 2):
                    gate_products(s - 1, 1 - u)
                wait(pe, x1_half, 2 * s)
                if first:
                    first_second_half()
                    ctx_pair()
                else:
                    attend_half(1, ctx_pair)
                if second:
                    gate_products(0, 0)
                    for n, tiles in enumerate((POOL_W, HB - POOL_W)):
                        pe.wait_ge(w_t[n], 32 * tiles)
                if at_least(s, 1):
                    wait(pe, out_half, 2 * s - 3)
                    before = 7 if second else 1
                    linear(1 - u, 0, range(before))
                    gated_transpose(s - 1)
                    linear(1 - u, 0, range(before, KD))
                if kind == "project" and u == 1:
                    wait(pe, exp_ready, TILES * (b + 1))
                    wait(pe, k_lo, g)
                    wait(pe, q_copied, g)
                    pe.wait_ge(ctx_lo, 4 * g + 4)
                    project(1, half(ps_score, 0))
                    project(0, half(ps_score, 1))
                if at_least(s, 1):
                    pe.wait_ge(h_lo, s)
                    lora(0)
                    if second:
                        pe.wait_ge(w_t[2], 32 * HB)
                    linear(1 - u, 1, range(KD))
                    lora(1)

            run_steps(pe, step)
            gate_products(STEPS - 1, 1)
            pe.wait_ge(out_half, 2 * STEPS - 3)
            linear(1, 0, range(6))
            gated_transpose(STEPS - 1)
            linear(1, 0, range(6, KD))
            pe.wait_ge(h_lo, STEPS)
            lora(0)
            linear(1, 1, range(KD))
            lora(1)


_INS = ["x", "ctx_1024", "g_xattn", "g_ffn", "L0_xattn_Wq", "L0_xattn_bq", "L0_xattn_Wk",
        "L0_xattn_bk", "L0_ffn_W", "L0_ffn_b", "L0_ffn_lora_A", "L0_ffn_lora_B", "L0_ffn_gate_w",
        "L0_ffn_gate_b"]
_OUTS = [((B, L, D), "float32")]


def kernel(**inputs):
    import numpy as _np
    import concourse.bacc as _bacc
    from concourse import mybir as _mybir
    from concourse.bass_utils import run_bass_kernel_spmd as _run

    nc = _bacc.Bacc("TRN2", target_bir_lowering=False, num_devices=1)
    arrays, args = {}, []
    for name in _INS:
        a = _np.ascontiguousarray(inputs[name])
        arrays[f"in_{name}_dram"] = a
        args.append(nc.dram_tensor(f"in_{name}_dram", a.shape, _mybir.dt.from_np(a.dtype),
                                   kind="ExternalInput").ap())
    for i, (shape, dtype) in enumerate(_OUTS):
        dt = _mybir.dt.from_np(_np.dtype(dtype))
        args.append(nc.dram_tensor(f"out_{i}_dram", shape, dt, kind="ExternalOutput").ap())
    flamingo_block(nc, *args)
    r = _run(nc, [arrays], core_ids=[0])
    return r.results[0]["out_0_dram"]
```
